# Optimizing a Trainium2 kernel written in Bass

```python
import numpy as np
import jax
import jax.numpy as jnp

def _softmax(x, axis=-1):
    return jax.nn.softmax(x, axis=axis)

def _gelu(x):
    return jax.nn.gelu(x, approximate=True)

def _silu(x):
    return jax.nn.silu(x)

def _sigmoid(x):
    return jax.nn.sigmoid(x)

def _layernorm(x, axis=-1, eps=1e-05):
    m = jnp.mean(x, axis=axis, keepdims=True)
    v = jnp.var(x, axis=axis, keepdims=True)
    return (x - m) / jnp.sqrt(v + eps)

def _scatter_add(tgt, idx, src, axis=0):
    return tgt.at[idx].add(src)

def _segment_sum(src, seg, n):
    return jax.ops.segment_sum(src, seg, n)
kernel_name = 'mk_recurrent_d1_jaxref_r8_11203b'

def setup_inputs(seed: int=0):
    np.random.seed(seed)
    _w = jnp.asarray

    def _L0_attn_setup():
        import jax, jax.numpy as jnp
        import numpy as np
        B, S, E, H = (2, 256, 512, 32)
        D = E // H
        ROPE_BASE = 10000.0
        MASK_VAL = -66504.0

        def _rope(x, cos, sin):
            x1, x2 = jnp.split(x, 2, axis=-1)
            return jnp.concatenate([x1 * cos - x2 * sin, x2 * cos + x1 * sin], axis=-1)
        key = jax.random.key(seed)
        k1, k2, k3, k4, k5 = jax.random.split(key, 5)
        return {'hidden_states': jax.random.normal(k1, (B, S, E), dtype=jnp.float32), 'qkv_w': jax.random.normal(k2, (E, 3 * E), dtype=jnp.float32) * 0.02, 'qkv_b': jax.random.normal(k3, (3 * E,), dtype=jnp.float32) * 0.02, 'out_w': jax.random.normal(k4, (E, E), dtype=jnp.float32) * 0.02, 'out_b': jax.random.normal(k5, (E,), dtype=jnp.float32) * 0.02}
    _L0_attn_in = _L0_attn_setup()

    def _L0_ffn_setup():
        import jax, jax.numpy as jnp
        import numpy as np
        LORA_SCALE = 16.0 / jnp.sqrt(16.0)
        TOP_K = 2
        key = jax.random.key(seed)
        k1, k2, k3, k4 = jax.random.split(key, 4)
        B_, S, D, O, E, R = (4, 256, 512, 512, 4, 16)
        x = jax.random.normal(k1, (B_, S, D), dtype=jnp.float32)
        router_w = jax.random.normal(k2, (E, D), dtype=jnp.float32) * 0.02
        A = jax.random.normal(k3, (E, R, D), dtype=jnp.float32) * 0.02
        B = jax.random.normal(k4, (O,), dtype=jnp.float32)
        B = jax.random.normal(k4, (E, O, R), dtype=jnp.float32) * 0.02
        return {'x': x, 'router_w': router_w, 'A': A, 'B': B}
    _L0_ffn_in = _L0_ffn_setup()
    _d = {'L0_attn_hidden_states': _L0_attn_in['hidden_states'], 'L0_attn_qkv_w': _L0_attn_in['qkv_w'], 'L0_attn_qkv_b': _L0_attn_in['qkv_b'], 'L0_attn_out_w': _L0_attn_in['out_w'], 'L0_attn_out_b': _L0_attn_in['out_b'], 'L0_ffn_router_w': _L0_ffn_in['router_w'], 'L0_ffn_A': _L0_ffn_in['A'], 'L0_ffn_B': _L0_ffn_in['B']}
    _x0 = _d['L0_attn_hidden_states']
    _d['L0_attn_hidden_states'] = jax.random.normal(jax.random.fold_in(jax.random.key(seed), 1), (4, 256, 512), dtype=_x0.dtype)
    del _x0
    return _d

def reference(L0_attn_hidden_states, L0_attn_qkv_w, L0_attn_qkv_b, L0_attn_out_w, L0_attn_out_b, L0_ffn_router_w, L0_ffn_A, L0_ffn_B):

    def _L0_attn_ref(hidden_states, qkv_w, qkv_b, out_w, out_b):
        import jax, jax.numpy as jnp
        import numpy as np
        B, S, E, H = (2, 256, 512, 32)
        D = E // H
        ROPE_BASE = 10000.0
        MASK_VAL = -66504.0

        def _rope(x, cos, sin):
            x1, x2 = jnp.split(x, 2, axis=-1)
            return jnp.concatenate([x1 * cos - x2 * sin, x2 * cos + x1 * sin], axis=-1)
        b, s, e = hidden_states.shape
        qkv = hidden_states @ qkv_w + qkv_b
        q, k, v = jnp.split(qkv, 3, axis=-1)
        q = q.reshape(b, s, H, D)
        k = k.reshape(b, s, H, D)
        v = v.reshape(b, s, H, D)
        half = D // 2
        inv_freq = 1.0 / ROPE_BASE ** (jnp.arange(0, half, dtype=jnp.float32) / half)
        ang = jnp.arange(s, dtype=jnp.float32)[:, None] * inv_freq[None, :]
        cos = jnp.cos(ang)[None, :, None, :]
        sin = jnp.sin(ang)[None, :, None, :]
        q = _rope(q, cos, sin)
        k = _rope(k, cos, sin)
        scale = 1.0 / jnp.sqrt(jnp.asarray(D, dtype=hidden_states.dtype))
        scores = jnp.einsum('bqhd,bkhd->bhqk', q, k) * scale
        causal = jnp.tril(jnp.ones((s, s), dtype=scores.dtype))
        scores = scores + (1.0 - causal) * MASK_VAL
        probs = jax.nn.softmax(scores, axis=-1)
        ctx = jnp.einsum('bhqk,bkhd->bqhd', probs, v).reshape(b, s, e)
        return ctx @ out_w + out_b

    def _L0_ffn_ref(x, router_w, A, B):
        import jax, jax.numpy as jnp
        import numpy as np
        LORA_SCALE = 16.0 / jnp.sqrt(16.0)
        TOP_K = 2
        D = x.shape[-1]
        flat = x.reshape(-1, D)
        logits = flat @ router_w.T
        topk_vals, topk_idx = jax.lax.top_k(logits, TOP_K)
        sparse = jnp.full_like(logits, -jnp.inf)
        rows = jnp.arange(logits.shape[0])[:, None]
        sparse = sparse.at[rows, topk_idx].set(topk_vals)
        gates = jax.nn.softmax(sparse, axis=-1)
        mid = jnp.einsum('tf,erf->ter', flat, A)
        all_deltas = jnp.einsum('ter,eor->teo', mid, B) * LORA_SCALE
        delta = jnp.einsum('te,teo->to', gates, all_deltas)
        return delta.reshape(*x.shape[:-1], -1)
    x = L0_attn_hidden_states
    xn = _layernorm(x, axis=-1)
    s = _L0_attn_ref(xn, L0_attn_qkv_w, L0_attn_qkv_b, L0_attn_out_w, L0_attn_out_b)
    g = _silu(_L0_ffn_ref(xn, L0_ffn_router_w, L0_ffn_A, L0_ffn_B))
    x = x + s * g
    return x

_drawn_inputs = setup_inputs


def setup_inputs(seed=0):
    import zlib

    import numpy as np

    out = dict(_drawn_inputs(seed))
    spreads = {}
    factors = {'L0_attn_qkv_w': 8.0,
     'L0_attn_qkv_b': 8.0,
     'L0_attn_out_w': 8.0,
     'L0_attn_out_b': 33.827,
     'L0_ffn_router_w': 8.0,
     'L0_ffn_A': 8.0,
     'L0_ffn_B': 8.0}
    for name, (base, spread) in spreads.items():
        noise = np.random.default_rng([zlib.crc32(name.encode()), seed]).standard_normal(out[name].shape)
        drawn = base * np.exp(spread * noise) if base else spread * noise
        out[name] = jnp.asarray(drawn.astype(out[name].dtype))
    for name, factor in factors.items():
        out[name] = (out[name] * factor).astype(out[name].dtype)
    return out
```

```python
from contextlib import ExitStack

import concourse.bass as bass
from concourse import mybir
from concourse.alu_op_type import AluOpType as ALU

F32 = mybir.dt.float32
F32R = mybir.dt.float32r
BF16 = mybir.dt.bfloat16
ACT = mybir.ActivationFunctionType
AX = mybir.AxisListType

P = 128
MASK = -66504.0


def plan(NB, NU):
    NG = NU // 2
    order = [("ln_stats", 0), ("ln_apply", 0), ("xt", 0, 0), ("xt", 0, 1)]
    order += [("proj", 0, t, w) for w in range(2) for t in range(2)]
    order += [("qkt", 0, t, w) for w in range(2) for t in range(2)]
    order += [("stack", 0, u) for u in range(NU)]
    order += [("proj", 0, t, c) for t in range(2) for c in (2, 3)]

    def fill(b, g):
        n, last, out = b + 1, b - 1, []
        if g == 0:
            if n < NB:
                out += [("ln_stats", n), ("ln_apply", n), ("xt", n, 0), ("xt", n, 1)]
                out += [("proj", n, 0, 0), ("proj", n, 1, 0), ("proj", n, 0, 1)]
            if 0 < b < NB:
                out += [("stack", b, NU - 2), ("stack", b, NU - 1)]
        if g == 1:
            if last >= 0:
                out += [("otok", last, h, t) for h in range(2) for t in range(2)]
                out += [("gate_a", last)]
            if n < NB:
                out += [("proj", n, 1, 1)]
                out += [("qkt", n, t, w) for w in range(2) for t in range(2)]
                out += [("stack", n, 0), ("stack", n, 1), ("proj", n, 0, 2)]
            if last >= 0:
                out += [("gate_b", last), ("gmt", last)]
        if g == 2:
            if last >= 0:
                out += [("ctxt", last, 0), ("delta", last, 0), ("wo", last, 0)]
            if n < NB:
                out += [("proj", n, 0, 3), ("proj", n, 1, 2), ("stack", n, 2), ("stack", n, 3)]
        if g == 3:
            if last >= 0:
                out += [("ctxt", last, 1), ("delta", last, 1), ("wo", last, 1)]
            if n < NB:
                out += [("proj", n, 1, 3), ("stack", n, 4), ("stack", n, 5)]
        return out

    for s in range(NB * NG + NG):
        b, g = s // NG, s % NG
        main = []
        if s < NB * NG:
            main += [("row", 2 * s)]
        if 1 <= s <= NB * NG:
            main += [("tt", 2 * s - 2)]
        if s < NB * NG:
            main += [("row", 2 * s + 1)]
        if 1 <= s <= NB * NG:
            main += [("pv", 2 * s - 2), ("tt", 2 * s - 1), ("ov", 2 * s - 2), ("pv", 2 * s - 1)]
        if s < NB * NG:
            main += [("msplit", s)]
        if 1 <= s <= NB * NG:
            main += [("ov", 2 * s - 1)]
        if s < NB * NG:
            main += [("mt", s)]
        more = fill(b, g)
        done = 0
        for i, m in enumerate(main):
            order.append(m)
            upto = len(more) * (i + 1) // len(main)
            order += more[done:upto]
            done = upto
        order += more[done:]
    return order


def bass_attention_times_silu_lora(nc, x, w_all, bias, w_out, experts_b, rope_cos, rope_sin, out):
    NB, S, E = x.shape
    H, D = 32, 16
    HALF = D // 2
    NE, R = 4, 16
    ER = NE * R
    NT = S // P
    KC = E // P
    NU = H // 4
    NG = NU // 2
    SCALE = 1.0 / D ** 0.5
    LORA_SCALE = 16.0 / 16.0 ** 0.5
    EPS = 1e-5
    WC = w_all.shape[1]
    VCUT = 18
    COLS = [(0, E), (E, 2 * E), (2 * E, 2 * E + VCUT * D), (2 * E + VCUT * D, WC)]
    MID = (H - VCUT) * D
    MASK_ID = 163.0
    MASK_TRI = MASK / SCALE / MASK_ID
    assert NT == 2 and WC == 3 * E + ER + NE and MASK_TRI == -1632.0

    ORDER = plan(NB, NU)
    nth, seen, misc_no = {}, {}, {}
    for step in ORDER:
        nth[step] = seen.get(step[0], 0)
        seen[step[0]] = nth[step] + 1
        if step[0] in ("xt", "proj", "qkt", "otok", "ctxt", "gmt", "delta", "wo", "mt"):
            misc_no[step] = len(misc_no)

    with ExitStack() as ctx:
        def sb(name, shape, dt=F32):
            return ctx.enter_context(nc.sbuf_tensor(name, shape, dt))

        def psum(name):
            return ctx.enter_context(nc.psum_tensor(name, [P, 512], F32))

        def sem(name):
            return ctx.enter_context(nc.semaphore(name))

        xs = sb("xs", [P, NB * NT, E])
        xn = sb("xn", [P, NT, E])
        ctx_n = xn
        x_hi = sb("x_hi", [P, NT, KC, P], F32R)
        x_lo = sb("x_lo", [P, NT, KC, P], F32R)
        w_hi = sb("w_hi", [P, KC, WC], F32R)
        w_lo = sb("w_lo", [P, KC, WC], F32R)
        wo_hi = sb("wo_hi", [P, KC, E], F32R)
        wo_lo = sb("wo_lo", [P, KC, E], F32R)
        bias_rows = sb("bias_rows", [2, WC + E], F32R)
        ones_rows = sb("ones_rows", [2, P], F32R)
        minus_row = sb("minus_row", [2, 1])
        expert_out = sb("expert_out", [ER, E])
        cos_t = sb("cos_t", [P, NT, D])
        sin_t = sb("sin_t", [P, NT, D])
        qk_rot = sb("qk_rot", [P, NT, 2, E])
        rope_sin_part = sb("rope_sin_part", [P, 2, E])
        parts = sb("parts", [P, 6, 4, S], BF16)
        part_rest = sb("part_rest", [P, E])
        stack = sb("stack", [P, 2, H, S], BF16)
        v_ones = sb("v_ones", [P, 2, NT, H, D + 1])
        probs = sb("probs", [P, 6, 512])
        o_t = sb("o_t", [P, NU, S])
        ctx_hi = sb("ctx_hi", [P, KC, P], F32R)
        ctx_lo = sb("ctx_lo", [P, KC, P], F32R)
        fin = sb("fin", [P, 2, E])
        ident = sb("ident", [P, P])
        ident_b = sb("ident_b", [P, P], BF16)
        mask_id = sb("mask_id", [P, P], BF16)
        tri_row = sb("tri_row", [P, P], BF16)
        tri_col = sb("tri_col", [P, P], BF16)
        ln_st = sb("ln_st", [P, NT, 6])
        ln_mv = sb("ln_mv", [P, NT, 2])
        ln_ve = sb("ln_ve", [P, NT, 1])
        ln_rs = sb("ln_rs", [P, NT, 1])
        neg_half = sb("neg_half", [P, NT, 1])
        mx = sb("mx", [P, 2, NT, 8])
        m_parts = sb("m_parts", [P, 2, NT, 3, 8], BF16)
        m_rest = sb("m_rest", [P, NT, 8])
        m_rows = sb("m_rows", [24, 2, S], BF16)
        rsum = sb("rsum", [P, 2, 16])
        ar = sb("ar", [P, 2, NT, ER + NE])
        before = sb("before", [P, NE, NE])
        g_gt = sb("g_gt", [P, NT, NE, NE])
        g_eq = sb("g_eq", [P, NT, NE, NE])
        g_rank = sb("g_rank", [P, NT, NE])
        g_max = sb("g_max", [P, NT, 1])
        g_exp = sb("g_exp", [P, NT, NE])
        g_sum = sb("g_sum", [P, NT, 1])
        gm = sb("gm", [P, NT, ER])
        gm_t = sb("gm_t", [ER, S])

        w_raw = stack[:, :, :, :].rearrange("p a h s -> p (a h s)").bitcast(F32)
        wo_raw = probs[:, :, :].rearrange("p a n -> p (a n)")[:, 0:KC * E].rearrange("p (k n) -> p k n", k=KC)
        bias_raw = qk_rot[0:2, :, :, :].rearrange("p a b n -> p (a b n)")
        bias_hi = o_t[0:2, :, :].rearrange("p a n -> p (a n)")
        w_at, at = [], 0
        for c0, c1 in ((0, E), (E, 2 * E), (2 * E, WC)):
            w_at.append((c0, c1, w_raw[:, at:at + KC * (c1 - c0)].rearrange("p (k n) -> p k n", k=KC)))
            at += KC * (c1 - c0)

        row_bank = [psum("row_bank0"), psum("row_bank1")]
        t_bank = [psum("t_bank0"), psum("t_bank1")]
        o_bank = [psum("o_bank0"), psum("o_bank1")]
        misc_bank = [psum("misc_bank0"), psum("misc_bank1")]

        x_in = [sem(f"x_in{b}") for b in range(NB)]
        w_in = [sem(f"w_in{i}") for i in range(3)]
        wo_in, bias_in, eb_in, rope_in = sem("wo_in"), sem("bias_in"), sem("eb_in"), sem("rope_in")
        ident_ready, masks_ready, v_ones_ready = sem("ident_ready"), sem("masks_ready"), sem("v_ones_ready")
        stack_ones = sem("stack_ones")
        w_hi_done, w_lo_done = sem("w_hi_done"), sem("w_lo_done")
        bias_step = sem("bias_step")
        dve_step = sem("dve_step")
        pool_step = sem("pool_step")
        stats_ready, rstd_ready, xn_ready = sem("stats_ready"), sem("rstd_ready"), sem("xn_ready")
        xh_ready, ar_v_ready = sem("xh_ready"), sem("ar_v_ready")
        misc_full = sem("misc_full")
        misc_free = [sem("misc_free0"), sem("misc_free1")]
        rope_done = sem("rope_done")
        qh_ready, parts_ready = sem("qh_ready"), sem("parts_ready")
        stack_in = [sem(f"stack_in{u}") for u in range(NU)]
        row_full, row_max = sem("row_full"), sem("row_max")
        mp_ready, m_copied = sem("mp_ready"), sem("m_copied")
        m_in = [sem("m_in0"), sem("m_in1")]
        t_full, exp_done = sem("t_full"), sem("exp_done")
        o_full, o_copied = sem("o_full"), sem("o_copied")
        o_zeroed = sem("o_zeroed")
        ch_ready = sem("ch_ready")
        gate_dl, gate_exp, gm_ready = sem("gate_dl"), sem("gate_exp"), sem("gm_ready")
        tanh_done, out_ready = sem("tanh_done"), sem("out_ready")
        stored = [sem("stored0"), sem("stored1")]

        def misc(step):
            return misc_bank[misc_no[step] % 2]

        def misc_freed(step):
            return misc_free[misc_no[step] % 2]

        def wait_misc_full(eng, step):
            eng.wait_ge(misc_full, misc_no[step] + 1)

        def wait_misc_free(eng, step):
            if misc_no[step] >= 2:
                eng.wait_ge(misc_freed(step), misc_no[step] // 2)

        def wait_misc_read(eng, step):
            eng.wait_ge(misc_freed(step), misc_no[step] // 2 + 1)

        rope_no = {step: i for i, step in enumerate(s for s in ORDER if s[0] == "proj" and s[3] < 2)}

        block = ctx.enter_context(nc.Block())

        @block.sync
        def _(sp):
            x_v = x.rearrange("b (t p) e -> b p t e", p=P)
            w_v = w_all.rearrange("(k p) n -> p k n", p=P)
            sp.dma_start(xs[:, 0:NT, :], x_v[0]).then_inc(x_in[0], 16)
            for i, (c0, c1, raw) in enumerate(w_at):
                sp.dma_start(raw, w_v[:, :, c0:c1]).then_inc(w_in[i], 16)
                if i == 0:
                    sp.dma_start(cos_t[:, :, :], rope_cos.rearrange("(t p) d -> p t d", p=P)).then_inc(rope_in, 16)
                    sp.dma_start(sin_t[:, :, :], rope_sin.rearrange("(t p) d -> p t d", p=P)).then_inc(rope_in, 16)
            for b in range(1, NB):
                sp.dma_start(xs[:, b * NT:(b + 1) * NT, :], x_v[b]).then_inc(x_in[b], 16)

            for step in ORDER:
                kind = step[0]
                if kind == "stack":
                    _, b, u = step
                    sp.wait_ge(parts_ready, 4 * (b + 1))
                    if b == 0 and u == 0:
                        sp.wait_ge(stack_ones, 1)
                    if b:
                        sp.wait_ge(t_full, 3 * (NU * (b - 1) + u + 1))
                    for slot, (qp, kp) in enumerate(((0, 0), (0, 1), (0, 2), (1, 0), (1, 1), (2, 0))):
                        sp.dma_start(stack[D * slot:D * (slot + 1), :, 4 * u:4 * u + 4, :],
                                     parts[D * u:D * (u + 1), qp:4 + kp:3 + kp - qp, :, :]).then_inc(stack_in[u], 16)
                if kind == "wo":
                    _, b, t = step
                    f = NT * b + t
                    sp.wait_ge(out_ready, f + 1)
                    sp.dma_start(out[b, t * P:(t + 1) * P, :], fin[:, f % 2, :]).then_inc(stored[f % 2], 16)
            for q in stored:
                sp.wait_ge(q, 16 * (NB * NT // 2))

        @block.gpsimd
        def _(pool):
            n = [0]

            def link(ins):
                n[0] += 1
                ins.then_inc(pool_step, 1)
                pool.wait_ge(pool_step, n[0])

            def masked(tile, value, op, step, mult):
                link(pool.memset(tile[:, :], value))
                return pool.affine_select(out=tile[:, :], in_=tile[:, :], compare_op=op, fill=0.0, base=0,
                                          pattern=[[step, tile.shape[1]]], channel_multiplier=mult)

            link(pool.memset(neg_half[:, :, :], -0.5))
            masked(ident, 1.0, ALU.is_equal, -1, 1).then_inc(ident_ready, 1)
            pool.memset(ones_rows[:, :].bitcast(F32), 1.0).then_inc(bias_step, 1)
            link(pool.memset(minus_row[:, :], -1.0))
            pool.affine_select(out=minus_row[:, :], in_=minus_row[:, :], compare_op=ALU.is_gt, fill=0.0, base=0,
                               pattern=[[1, 1]], channel_multiplier=1).then_inc(bias_step, 1)
            masked(ident_b, 1.0, ALU.is_equal, -1, 1).then_inc(masks_ready, 1)
            masked(mask_id, MASK_ID, ALU.is_equal, -1, 1).then_inc(masks_ready, 1)
            masked(tri_row, MASK_TRI, ALU.is_gt, -1, 1).then_inc(masks_ready, 1)
            masked(tri_col, MASK_TRI, ALU.is_gt, 1, -1).then_inc(masks_ready, 1)
            pool.memset(v_ones[:, :, :, :, D:D + 1].rearrange("p a t h d -> p (a t h) d"), 1.0).then_inc(v_ones_ready, 1)

            for step in ORDER:
                kind = step[0]
                if kind == "ln_stats":
                    pool.wait_ge(stats_ready, NT * (nth[step] + 1))
                    link(pool.tensor_scalar(ln_ve[:, :, :], ln_mv[:, :, 1:2], EPS, None, ALU.add))
                    pool.tensor_tensor(ln_rs[:, :, :], ln_ve[:, :, :], neg_half[:, :, :], ALU.pow).then_inc(rstd_ready, 1)
                if step == ("proj", 0, 0, 0):
                    pool.wait_ge(w_lo_done, 3)
                    pool.memset(stack[96:128, 1, :, :], 1.0).then_inc(stack_ones, 1)
                    pool.wait_ge(stack_ones, 1)
                if kind == "proj" and step[3] < 2:
                    _, b, t, w = step
                    r = rope_no[step]
                    wait_misc_read(pool, step)
                    pool.tensor_tensor(qk_rot[:, t, w, :], qk_rot[:, t, w, :], rope_sin_part[:, r % 2, :],
                                       ALU.add).then_inc(rope_done, 1)
                if kind == "wo":
                    _, b, t = step
                    f = NT * b + t
                    wait_misc_read(pool, step)
                    pool.tensor_tensor(fin[:, f % 2, :], fin[:, f % 2, :], xs[:, f, :], ALU.add).then_inc(out_ready, 1)

        @block.scalar
        def _(act):
            act.dma_start(bias_raw[0:1, :], bias).then_inc(bias_in, 16)
            act.dma_start(bias_raw[1:2, :], bias).then_inc(bias_in, 16)
            act.dma_start(wo_raw, w_out.rearrange("(k p) n -> p k n", p=P)).then_inc(wo_in, 16)
            act.dma_start(expert_out[:, :], experts_b).then_inc(eb_in, 16)

            def weights_hi(i):
                c0, c1, raw = w_at[i]
                act.wait_ge(w_in[i], 16)
                nc.scalar.activation(w_hi[:, :, c0:c1], raw, ACT.Copy).then_inc(w_hi_done, 1)

            weights_hi(0)
            act.wait_ge(bias_in, 32)
            nc.scalar.activation(bias_hi.bitcast(F32R), bias_raw, ACT.Copy).then_inc(bias_step, 1)
            for step in ORDER:
                kind = step[0]
                if step == ("proj", 0, 0, 0):
                    weights_hi(1)
                    weights_hi(2)
                    act.wait_ge(wo_in, 16)
                    nc.scalar.activation(wo_hi[:, :, :], wo_raw, ACT.Copy).then_inc(w_hi_done, 1)
                if kind == "xt":
                    _, b, t = step
                    wait_misc_full(act, step)
                    if b:
                        wait_misc_full(act, ("proj", b - 1, t, 3))
                    nc.scalar.activation(x_hi[:, t, :, :], misc(step)[:, :].rearrange("p (k n) -> p k n", k=KC),
                                         ACT.Copy).then_inc(xh_ready, 1)
                if kind == "qkt":
                    _, b, t, w = step
                    wait_misc_full(act, step)
                    if b and nth[step] % 4 == 0:
                        for u in range(NU):
                            act.wait_ge(stack_in[u], 96 * b)
                    nc.scalar.activation(parts[:, 3 * w, :, t * P:(t + 1) * P],
                                         misc(step)[:, :].rearrange("p (g n) -> p g n", g=4),
                                         ACT.Copy).then_inc(qh_ready, 1)
                if kind == "proj" and step[3] >= 2:
                    _, b, t, c = step
                    wait_misc_full(act, step)
                    if b >= 2:
                        act.wait_ge(o_full, NU * (b - 1))
                    elif b == 0:
                        act.wait_ge(v_ones_ready, 1)
                    h0, h1 = (0, VCUT) if c == 2 else (VCUT, H)
                    cols = (h1 - h0) * D
                    if c == 3:
                        nc.scalar.activation(ar[:, b % 2, t, :], misc(step)[:, cols:cols + ER + NE],
                                             ACT.Copy).then_inc(ar_v_ready, 1)
                    nc.scalar.activation(v_ones[:, b % 2, t, h0:h1, 0:D],
                                         misc(step)[:, 0:cols].rearrange("p (h d) -> p h d", d=D),
                                         ACT.Copy).then_inc(misc_freed(step), 1)
                if kind == "mt":
                    s = step[1]
                    b, g = s // NG, s % NG
                    wait_misc_full(act, step)
                    if s >= 2:
                        act.wait_ge(m_in[s % 2], 16 * (s // 2))
                    nc.scalar.activation(m_rows[:, s % 2, :], misc(step)[0:24, 0:P].bitcast(BF16),
                                         ACT.Copy).then_inc(misc_freed(step), 1)
                    wait_misc_read(act, step)
                    if b:
                        act.wait_ge(t_full, 3 * (NU * (b - 1) + 2 * g + 2))
                    act.dma_start(stack[96:99, 0, 8 * g:8 * g + 8, :], m_rows[:, s % 2, :]).then_inc(m_in[s % 2], 16)
                if kind == "tt":
                    U = step[1]
                    for i in range(3):
                        n = 3 * U + i
                        act.wait_ge(t_full, n + 1)
                        if U >= 2 and i == 0:
                            act.wait_ge(o_full, U - 1)
                        if U == 0 and i == 0:
                            act.wait_ge(w_lo_done, 4)
                        nc.scalar.activation(probs[:, n % 6, :], t_bank[n % 2][:, :], ACT.Exp,
                                             scale=SCALE).then_inc(exp_done, 1)
                if kind == "ov":
                    U = step[1]
                    b, u = U // NU, U % NU
                    act.wait_ge(o_full, U + 1)
                    if b:
                        wait_misc_full(act, ("otok", b - 1, u // 4, 1))
                    elif u == 0:
                        act.wait_ge(bias_step, 4)
                    nc.scalar.activation(o_t[:, u, :], o_bank[U % 2][:, 0:S], ACT.Copy).then_inc(o_copied, 1)
                if kind == "ctxt":
                    _, b, t = step
                    wait_misc_full(act, step)
                    f = NT * b + t
                    if f:
                        wait_misc_full(act, ("wo", (f - 1) // NT, (f - 1) % NT))
                    nc.scalar.activation(ctx_hi[:, :, :], misc(step)[:, :].rearrange("p (k n) -> p k n", k=KC),
                                         ACT.Copy).then_inc(ch_ready, 1)
                if kind == "gate_a":
                    b = step[1]
                    act.wait_ge(gate_dl, b + 1)
                    nc.scalar.activation(g_exp[:, :, :], g_exp[:, :, :], ACT.Exp).then_inc(gate_exp, 1)
                if kind == "delta":
                    _, b, t = step
                    f = NT * b + t
                    wait_misc_full(act, step)
                    if f >= 2:
                        act.wait_ge(stored[f % 2], 16 * (f // 2))
                    nc.scalar.activation(fin[:, f % 2, :], misc(step)[:, :], ACT.Tanh,
                                         scale=0.5).then_inc(tanh_done, 1)

        @block.vector
        def _(dve):
            n = [0]

            def link(ins):
                n[0] += 1
                ins.then_inc(dve_step, 1)
                dve.wait_ge(dve_step, n[0])

            def weights_lo(i):
                c0, c1, raw = w_at[i]
                dve.wait_ge(w_hi_done, i + 1)
                dve.tensor_tensor(w_lo[:, :, c0:c1], raw, w_hi[:, :, c0:c1].bitcast(F32),
                                  ALU.subtract).then_inc(w_lo_done, 1)

            link(dve.memset(before[:, :, :], 0.0))
            for e in range(1, NE):
                last = dve.memset(before[:, e, 0:e], 1.0)
            link(last)
            link(dve.memset(bias_rows[:, :].bitcast(F32), 0.0))
            for bank in o_bank:
                last = dve.memset(bank[:, 0:S], 0.0)
            last.then_inc(o_zeroed, 1)

            for step in ORDER:
                kind = step[0]
                if step == ("proj", 0, 0, 0):
                    weights_lo(0)
                    dve.wait_ge(bias_step, 3)
                    for o, c0, c1 in ((0, 0, 3 * E), (WC, 3 * E, 4 * E)):
                        last = dve.scalar_tensor_tensor(bias_rows[:, o:o + c1 - c0], bias_hi[:, c0:c1],
                                                        minus_row[:, 0:1], bias_raw[:, c0:c1], ALU.mult, ALU.add)
                    last.then_inc(bias_step, 1)
                    weights_lo(1)
                    weights_lo(2)
                    dve.wait_ge(rope_in, 32)
                    dve.wait_ge(bias_step, 4)
                if step == ("proj", 0, 0, 2):
                    dve.wait_ge(w_hi_done, 4)
                    dve.tensor_tensor(wo_lo[:, :, :], wo_raw, wo_hi[:, :, :].bitcast(F32),
                                      ALU.subtract).then_inc(w_lo_done, 1)
                if kind == "ln_stats":
                    b = step[1]
                    dve.wait_ge(x_in[b], 16)
                    for t in range(NT):
                        last = dve.bn_stats(ln_st[:, t, :], xs[:, NT * b + t, :])
                    link(last)
                    for t in range(NT):
                        dve.bn_aggr(ln_mv[:, t, :], ln_st[:, t, :]).then_inc(stats_ready, 1)
                if kind == "ln_apply":
                    b = step[1]
                    dve.wait_ge(rstd_ready, b + 1)
                    for t in range(NT):
                        dve.tensor_scalar(xn[:, t, :], xs[:, NT * b + t, :], ln_mv[:, t, 0:1], ln_rs[:, t, 0:1],
                                          ALU.subtract, ALU.mult).then_inc(xn_ready, 1)
                if kind == "xt":
                    _, b, t = step
                    dve.wait_ge(xh_ready, nth[step] + 1)
                    dve.tensor_tensor(x_lo[:, t, :, :], misc(step)[:, :].rearrange("p (k n) -> p k n", k=KC),
                                      x_hi[:, t, :, :].bitcast(F32), ALU.subtract).then_inc(misc_freed(step), 1)
                if kind == "proj" and step[3] < 2:
                    _, b, t, w = step
                    r = rope_no[step]
                    wait_misc_full(dve, step)
                    if r >= 2:
                        dve.wait_ge(rope_done, r - 1)
                    q = misc(step)[:, :].rearrange("p (h d) -> p h d", d=D)
                    dve.tensor_tensor(qk_rot[:, t, w, :].rearrange("p (h d) -> p h d", d=D), q,
                                      cos_t[:, t:t + 1, :].broadcast_to([P, H, D]), ALU.mult)
                    dve.tensor_tensor(
                        rope_sin_part[:, r % 2, :].rearrange("p (h a d) -> p h a d", a=2, d=HALF),
                        misc(step)[:, :].rearrange("p (h a d) -> p h a d", a=2, d=HALF)[:, :, ::-1, :],
                        sin_t[:, t, :].rearrange("p (a d) -> p a d", a=2).unsqueeze(1).broadcast_to([P, H, 2, HALF]),
                        ALU.mult).then_inc(misc_freed(step), 1)
                if kind == "qkt":
                    _, b, t, w = step
                    r = nth[step]
                    dve.wait_ge(qh_ready, r + 1)
                    if r:
                        dve.wait_ge(parts_ready, r)
                    rest = part_rest[:, :].rearrange("p (g n) -> p g n", g=4)
                    pw = parts[:, 3 * w:3 * w + 3, :, t * P:(t + 1) * P]
                    dve.tensor_tensor(rest, misc(step)[:, :].rearrange("p (g n) -> p g n", g=4), pw[:, 0, :, :],
                                      ALU.subtract).then_inc(misc_freed(step), 1)
                    wait_misc_read(dve, step)
                    link(dve.tensor_copy(pw[:, 1, :, :], rest))
                    dve.tensor_tensor(pw[:, 2, :, :], rest, pw[:, 1, :, :], ALU.subtract).then_inc(parts_ready, 1)
                if kind == "row":
                    U = step[1]
                    s, o = U // 2, 4 * (U % 2)
                    m = mx[:, s % 2, :, :]
                    for i in range(3):
                        n_ = 3 * U + i
                        dve.wait_ge(row_full, n_ + 1)
                        bank = row_bank[n_ % 2][:, :]
                        if i == 0:
                            dve.tensor_reduce(m[:, 0, o:o + 4], bank.rearrange("p (h n) -> p h n", h=4), AX.X,
                                              ALU.max).then_inc(row_max, 1)
                        else:
                            dve.tensor_reduce(m[:, 1, o + 2 * i - 2:o + 2 * i], bank.rearrange("p (h n) -> p h n", h=2),
                                              AX.X, ALU.max).then_inc(row_max, 1)
                if kind == "msplit":
                    s = step[1]
                    dve.wait_ge(row_max, 6 * (s + 1))
                    if s >= 2:
                        wait_misc_full(dve, ("mt", s - 2))
                    m, mp = mx[:, s % 2, :, :], m_parts[:, s % 2, :, :, :]
                    link(dve.tensor_scalar(mp[:, :, 0, :], m, -1.0, None, ALU.mult))
                    link(dve.scalar_tensor_tensor(m_rest[:, :, :], m, -1.0, mp[:, :, 0, :], ALU.mult, ALU.subtract))
                    link(dve.tensor_copy(mp[:, :, 1, :], m_rest[:, :, :]))
                    dve.tensor_tensor(mp[:, :, 2, :], m_rest[:, :, :], mp[:, :, 1, :],
                                      ALU.subtract).then_inc(mp_ready, 1)
                if kind == "otok":
                    _, b, half, t = step
                    wait_misc_full(dve, step)
                    o = misc(step)[:, :].rearrange("p (h d) -> p h d", d=2 * D)
                    link(dve.reciprocal(rsum[:, misc_no[step] % 2, :].rearrange("p (h d) -> p h d", d=1), o[:, :, D:D + 1]))
                    dve.tensor_tensor(
                        ctx_n[:, t, half * 256:(half + 1) * 256].rearrange("p (h d) -> p h d", d=D), o[:, :, 0:D],
                        rsum[:, misc_no[step] % 2, :].rearrange("p (h d) -> p h d", d=1).broadcast_to([P, 16, D]),
                        ALU.mult).then_inc(misc_freed(step), 1)
                if kind == "ctxt":
                    _, b, t = step
                    dve.wait_ge(ch_ready, nth[step] + 1)
                    dve.tensor_tensor(ctx_lo[:, :, :], misc(step)[:, :].rearrange("p (k n) -> p k n", k=KC),
                                      ctx_hi[:, :, :].bitcast(F32), ALU.subtract).then_inc(misc_freed(step), 1)
                if kind == "gate_a":
                    b = step[1]
                    dve.wait_ge(ar_v_ready, NT * (b + 1))
                    lg = ar[:, b % 2, :, ER:ER + NE]
                    for t in range(NT):
                        of_j = lg[:, t:t + 1, :].broadcast_to([P, NE, NE])
                        of_e = lg[:, t, :].unsqueeze(2).broadcast_to([P, NE, NE])
                        dve.tensor_tensor(g_gt[:, t, :, :], of_j, of_e, ALU.is_gt)
                        last = dve.tensor_tensor(g_eq[:, t, :, :], of_j, of_e, ALU.is_equal)
                    link(last)
                    for t in range(NT):
                        last = dve.tensor_tensor(g_eq[:, t, :, :], g_eq[:, t, :, :], before[:, :, :], ALU.mult)
                    link(last)
                    link(dve.tensor_tensor(g_gt[:, :, :, :], g_gt[:, :, :, :], g_eq[:, :, :, :], ALU.add))
                    dve.tensor_reduce(g_rank[:, :, :], g_gt[:, :, :, :], AX.X, ALU.add)
                    link(dve.tensor_reduce(g_max[:, :, :], lg, AX.X, ALU.max))
                    dve.tensor_tensor(g_exp[:, :, :], lg, g_max[:, :, :].broadcast_to([P, NT, NE]),
                                      ALU.subtract).then_inc(gate_dl, 1)
                if kind == "gate_b":
                    b = step[1]
                    dve.wait_ge(gate_exp, b + 1)
                    link(dve.scalar_tensor_tensor(g_exp[:, :, :], g_rank[:, :, :], 2.0, g_exp[:, :, :], ALU.is_lt,
                                                  ALU.mult))
                    link(dve.tensor_reduce(g_sum[:, :, :], g_exp[:, :, :], AX.X, ALU.add))
                    link(dve.reciprocal(g_sum[:, :, :], g_sum[:, :, :]))
                    link(dve.scalar_tensor_tensor(g_exp[:, :, :], g_exp[:, :, :], LORA_SCALE,
                                                  g_sum[:, :, :].broadcast_to([P, NT, NE]), ALU.mult, ALU.mult))
                    for t in range(NT):
                        last = dve.tensor_tensor(gm[:, t, :].rearrange("p (e r) -> p e r", r=R),
                                                 ar[:, b % 2, t, 0:ER].rearrange("p (e r) -> p e r", r=R),
                                                 g_exp[:, t, :].unsqueeze(2).broadcast_to([P, NE, R]), ALU.mult)
                    last.then_inc(gm_ready, 1)
                if kind == "gmt":
                    wait_misc_full(dve, step)
                    dve.tensor_copy(gm_t[:, :], misc(step)[0:ER, 0:S]).then_inc(misc_freed(step), 1)
                if kind == "delta":
                    _, b, t = step
                    f = NT * b + t
                    dve.wait_ge(tanh_done, f + 1)
                    dve.scalar_tensor_tensor(fin[:, f % 2, :], fin[:, f % 2, :], 1.0, misc(step)[:, :], ALU.add,
                                             ALU.mult).then_inc(misc_freed(step), 1)
                if kind == "wo":
                    _, b, t = step
                    f = NT * b + t
                    wait_misc_full(dve, step)
                    wait_misc_read(dve, ("delta", b, t))
                    dve.scalar_tensor_tensor(fin[:, f % 2, :], fin[:, f % 2, :], 0.5, misc(step)[:, :], ALU.mult,
                                             ALU.mult).then_inc(misc_freed(step), 1)

        @block.tensor
        def _(pe):
            def three_passes(bank, cols, hi, lo, rhs_hi, rhs_lo, bias_at):
                for k in range(KC):
                    for a, w in ((hi, rhs_hi), (hi, rhs_lo), (lo, rhs_hi)):
                        pe.matmul(bank[:, 0:cols], a[:, k, :], w[:, k, :], start=(k == 0 and a is hi and w is rhs_hi),
                                  stop=False)
                return pe.matmul(bank[:, 0:cols], ones_rows[:, :], bias_rows[:, bias_at:bias_at + cols],
                                 start=False, stop=True)

            for step in ORDER:
                kind = step[0]
                if step in misc_no:
                    wait_misc_free(pe, step)
                if kind == "xt":
                    _, b, t = step
                    if b == 0 and t == 0:
                        pe.wait_ge(ident_ready, 1)
                    pe.wait_ge(xn_ready, nth[step] + 1)
                    for k in range(KC):
                        last = pe.transpose(misc(step)[:, k * P:(k + 1) * P], xn[:, t, k * P:(k + 1) * P], ident[:, :])
                    last.then_inc(misc_full, 1)
                if kind == "proj":
                    _, b, t, c = step
                    wait_misc_read(pe, ("xt", b, t))
                    if b == 0:
                        pe.wait_ge(w_lo_done, min(c, 2) + 1)
                        pe.wait_ge(bias_step, 4)
                    c0, c1 = COLS[c]
                    three_passes(misc(step), c1 - c0, x_hi[:, t, :, :], x_lo[:, t, :, :], w_hi[:, :, c0:c1],
                                 w_lo[:, :, c0:c1], c0).then_inc(misc_full, 1)
                if kind == "qkt":
                    _, b, t, w = step
                    pe.wait_ge(rope_done, rope_no[("proj", b, t, w)] + 1)
                    for g in range(4):
                        last = pe.transpose(misc(step)[:, g * P:(g + 1) * P], qk_rot[:, t, w, g * P:(g + 1) * P],
                                            ident[:, :])
                    last.then_inc(misc_full, 1)
                if kind == "row":
                    U = step[1]
                    b, u = U // NU, U % NU
                    pe.wait_ge(stack_in[u], 96 * (b + 1))
                    if U == 0:
                        pe.wait_ge(masks_ready, 4)
                    for i in range(3):
                        n = 3 * U + i
                        if n >= 2:
                            pe.wait_ge(row_max, n - 1)
                        heads = range(4) if i == 0 else range(2 * i - 2, 2 * i)
                        t = 0 if i == 0 else 1
                        bank = row_bank[n % 2][:, :].rearrange("p (h n) -> p h n", h=len(heads))
                        width = 512 // len(heads)
                        pe.matmul(bank[:, :, t * P:(t + 1) * P], tri_row[:, :],
                                  mask_id[:, :].unsqueeze(1).broadcast_to([P, len(heads), P]), start=True, stop=False,
                                  skip_group_check=True)
                        for j, h in enumerate(heads):
                            last = pe.matmul(bank[:, j, :], stack[0:96, 0, 4 * u + h, t * P:(t + 1) * P],
                                             stack[0:96, 1, 4 * u + h, 0:width], start=False, stop=True,
                                             skip_group_check=True)
                        last.then_inc(row_full, 1)
                if kind == "mt":
                    s = step[1]
                    pe.wait_ge(mp_ready, s + 1)
                    for t in range(NT):
                        last = pe.transpose(misc(step)[0:24, t * 64:(t + 1) * 64].bitcast(BF16),
                                            m_parts[:, s % 2, t, :, :].rearrange("p a h -> p (a h)"), ident_b[:, :])
                    last.then_inc(misc_full, 1)
                if kind == "tt":
                    U = step[1]
                    b, u = U // NU, U % NU
                    s = U // 2
                    pe.wait_ge(m_in[s % 2], 16 * (s // 2 + 1))
                    for i in range(3):
                        n = 3 * U + i
                        if n >= 2:
                            pe.wait_ge(exp_done, n - 1)
                        heads = range(4) if i == 2 else range(2 * i, 2 * i + 2)
                        kb, q0 = (1, P) if i == 2 else (0, 0)
                        bank = t_bank[n % 2][:, :].rearrange("p (h n) -> p h n", h=len(heads))
                        pe.matmul(bank[:, :, 0:P], tri_col[:, :],
                                  mask_id[:, :].unsqueeze(1).broadcast_to([P, len(heads), P]), start=True, stop=False,
                                  skip_group_check=True)
                        for j, h in enumerate(heads):
                            last = pe.matmul(bank[:, j, :], stack[0:99, 1, 4 * u + h, kb * P:(kb + 1) * P],
                                             stack[0:99, 0, 4 * u + h, q0:S], start=False, stop=True,
                                             skip_group_check=True)
                        last.then_inc(t_full, 1)
                if kind == "pv":
                    U = step[1]
                    b, u = U // NU, U % NU
                    pe.wait_ge(exp_done, 3 * U + 3)
                    if u == 0:
                        for t in range(NT):
                            for c in (2, 3):
                                wait_misc_read(pe, ("proj", b, t, c))
                    if U == 0:
                        pe.wait_ge(o_zeroed, 1)
                    if U >= 2:
                        pe.wait_ge(o_copied, U - 1)
                    ob = o_bank[U % 2]
                    for kb in range(2):
                        for h in range(4):
                            n = 3 * U + (2 if kb else h // 2)
                            width = S - kb * P
                            at = h * width if kb else (h % 2) * width
                            last = pe.matmul(ob[32 * h:32 * h + D + 1, kb * P:S], v_ones[:, b % 2, kb, 8 * h + u, :],
                                             probs[:, n % 6, at:at + width], start=(kb == 0), stop=(kb == 1),
                                             skip_group_check=True)
                    last.then_inc(o_full, 1)
                if kind == "otok":
                    _, b, half, t = step
                    pe.wait_ge(o_copied, NU * b + 4 * half + 4)
                    for j in range(4):
                        last = pe.transpose(misc(step)[:, j * P:(j + 1) * P],
                                            o_t[:, 4 * half + j, t * P:(t + 1) * P], ident[:, :])
                    last.then_inc(misc_full, 1)
                if kind == "ctxt":
                    _, b, t = step
                    for half in range(2):
                        wait_misc_read(pe, ("otok", b, half, t))
                    for k in range(KC):
                        last = pe.transpose(misc(step)[:, k * P:(k + 1) * P], ctx_n[:, t, k * P:(k + 1) * P],
                                            ident[:, :])
                    last.then_inc(misc_full, 1)
                if kind == "gmt":
                    b = step[1]
                    pe.wait_ge(gm_ready, b + 1)
                    for t in range(NT):
                        last = pe.transpose(misc(step)[0:ER, t * P:(t + 1) * P], gm[:, t, :], ident[:, :])
                    last.then_inc(misc_full, 1)
                if kind == "delta":
                    _, b, t = step
                    wait_misc_read(pe, ("gmt", b))
                    if b == 0:
                        pe.wait_ge(eb_in, 16)
                    pe.matmul(misc(step)[:, :], gm_t[:, t * P:(t + 1) * P], expert_out[:, :], start=True,
                              stop=True).then_inc(misc_full, 1)
                if kind == "wo":
                    _, b, t = step
                    wait_misc_read(pe, ("ctxt", b, t))
                    if b == 0:
                        pe.wait_ge(w_lo_done, 4)
                    three_passes(misc(step), E, ctx_hi, ctx_lo, wo_hi, wo_lo, WC).then_inc(misc_full, 1)


def kernel(L0_attn_hidden_states, L0_attn_qkv_w, L0_attn_qkv_b, L0_attn_out_w, L0_attn_out_b, L0_ffn_router_w,
           L0_ffn_A, L0_ffn_B):
    import numpy as np
    import concourse.bacc as bacc
    from concourse.bass_utils import run_bass_kernel_spmd

    x = np.ascontiguousarray(L0_attn_hidden_states)
    NB, S, E = x.shape
    H, D = 32, 16
    w_all = np.concatenate([L0_attn_qkv_w, np.transpose(L0_ffn_A.reshape(-1, E)), np.transpose(L0_ffn_router_w)], axis=1)
    bias = np.concatenate([L0_attn_qkv_b, L0_attn_out_b])[None, :]
    w_out = L0_attn_out_w.reshape(4, 8, D, E).transpose(1, 0, 2, 3).reshape(E, E)
    experts_b = np.transpose(L0_ffn_B, (0, 2, 1)).reshape(-1, E)
    half = D // 2
    inv_freq = (1.0 / np.float32(10000.0) ** (np.arange(half, dtype=np.float32) / np.float32(half))).astype(np.float32)
    ang = np.arange(S, dtype=np.float32)[:, None] * inv_freq[None, :]
    cos, sin = np.cos(ang).astype(np.float32), np.sin(ang).astype(np.float32)
    arrays = {
        "in_x": x, "in_w_all": w_all, "in_bias": bias, "in_w_out": w_out, "in_experts_b": experts_b,
        "in_rope_cos": np.concatenate([cos, cos], axis=1), "in_rope_sin": np.concatenate([-sin, sin], axis=1),
    }
    arrays = {k: np.ascontiguousarray(v) for k, v in arrays.items()}
    nc = bacc.Bacc("TRN2", target_bir_lowering=False, num_devices=1)
    args = [nc.dram_tensor(k, v.shape, mybir.dt.from_np(v.dtype), kind="ExternalInput").ap() for k, v in arrays.items()]
    out = nc.dram_tensor("out_0", x.shape, F32, kind="ExternalOutput").ap()
    bass_attention_times_silu_lora(nc, *args, out)
    r = run_bass_kernel_spmd(nc, [arrays], core_ids=[0])
    return r.results[0]["out_0"]
```

```python
from contextlib import ExitStack

import concourse.bass as bass
from concourse import mybir
from concourse.alu_op_type import AluOpType as ALU

F32 = mybir.dt.float32
F32R = mybir.dt.float32r
BF16 = mybir.dt.bfloat16
ACT = mybir.ActivationFunctionType
AX = mybir.AxisListType

P = 128
MASK = -66504.0


ATTENTION = {
    ("row", 0): -9, ("row", 1): 5, ("row", 2): 8, ("row", 3): 35, ("row", 4): 38, ("row", 5): 59,
    ("msplit",): 75, ("mt",): 89, ("tt", 0): 122, ("tt", 1): 125, ("tt", 2): 135, ("tt", 3): 154,
    ("pv", 0): 159, ("ov", 0): 165, ("tt", 4): 174, ("tt", 5): 182, ("pv", 1): 203, ("ov", 1): 215,
}
ROW = {
    ("ln_stats", 0): -400, ("ln_stats", 1): -397, ("ln_apply", 0): -394, ("ln_apply", 1): -383, ("xt", 0): -371,
    ("xt", 1): -358, ("proj", 0, 0): (-342, 6), ("proj", 1, 0): (-332, 1), ("proj", 0, 1): (-320, 4),
    ("proj", 1, 1): (-307, 1), ("qkt", 1, 0): -282, ("qkt", 0, 1): -274, ("qkt", 0, 0): -263,
    ("qkt", 1, 1): -261, ("stack", 1): -250, ("proj", 0, 3): (-250, 2), ("proj", 0, 2): (-227, 1),
    ("stack", 0): -141, ("stack", 4): -130, ("stack", 2): -90, ("proj", 1, 3): (-86, 5),
    ("proj", 1, 2): (-58, 6), ("stack", 5): 12, ("stack", 3): 29, ("stack", 6): 72, ("stack", 7): 85,
    ("gate_a",): 323, ("gate_b",): 331, ("gmt",): 416, ("otok", 0, 0): 496, ("otok", 0, 1): 525,
    ("otok", 1, 0): 527, ("otok", 1, 1): 584, ("delta", 0): 599, ("ctxt", 0): 627, ("wo", 0): (673, 8),
    ("ctxt", 1): 698, ("delta", 1): 726, ("wo", 1): (788, 2),
}
FIRST = {
    ("ln_stats", 0): -1002, ("bias",): -995, ("ln_apply", 0): -994, ("ln_stats", 1): -992,
    ("ln_apply", 1): -992, ("xt", 0): -992, ("weights", 0): -985, ("weights", 1): -983, ("weights", 2): -966,
    ("xt", 1): -964, ("weights", 3): -955, ("proj", 0, 0): (-953, 4), ("weights", 4): -937,
    ("weights", 5): -929, ("proj", 1, 0): (-915, 6), ("proj", 0, 1): (-887, 4), ("qkt", 0, 0): -847,
    ("proj", 1, 1): (-845, 1), ("qkt", 0, 1): -839, ("qkt", 1, 0): -828, ("proj", 0, 2): (-820, 8),
    ("qkt", 1, 1): -803, ("stack", 0): -802, ("stack", 6): -801, ("stack", 1): -797, ("stack", 2): -797,
    ("stack", 5): -787, ("stack", 7): -769, ("proj", 1, 2): (-766, 1), ("weights", 6): -761, ("stack", 4): -747,
    ("stack", 3): -735, ("proj", 0, 3): (-711, 1), ("proj", 1, 3): (-686, 3), ("weights", 7): -597,
}
LAST = {
    ("gate_a",): 90, ("gate_b",): 93, ("otok", 0, 0): 357, ("otok", 0, 1): 386, ("gmt",): 453,
    ("otok", 1, 0): 530, ("otok", 1, 1): 591, ("ctxt", 0): 605, ("delta", 0): 606, ("wo", 0): (623, 1),
    ("ctxt", 1): 629, ("delta", 1): 631, ("wo", 1): (671, 1),
}


def plan(NB, NU):
    NG = NU // 2
    at = {}
    for s in range(NB * NG):
        for name, tick in ATTENTION.items():
            kind, i = name[0], name[1:]
            if kind in ("row", "tt"):
                step = (kind, 6 * s + i[0])
            elif kind in ("pv", "ov"):
                step = (kind, 2 * s + i[0])
            else:
                step = (kind, s)
            at[step] = 100 * s + tick
    for b in range(NB):
        ticks = dict(ROW)
        if b == 0:
            ticks.update(FIRST)
        if b == NB - 1:
            ticks.update(LAST)
        for name, tick in ticks.items():
            step = name[:1] + (b,) + name[1:]
            if name[0] in ("proj", "wo"):
                for k in range(4):
                    at[step + (k,)] = 100 * NG * b + tick[0] + tick[1] * k
            else:
                at[step] = 100 * NG * b + tick
    return sorted(at, key=at.get)


def bass_attention_times_silu_lora(nc, x, w_all, bias, w_out, experts_b, rope_cos, rope_sin, out):
    NB, S, E = x.shape
    H, D = 32, 16
    HALF = D // 2
    NE, R = 4, 16
    ER = NE * R
    NT = S // P
    KC = E // P
    NU = H // 4
    NG = NU // 2
    SCALE = 1.0 / D ** 0.5
    LORA_SCALE = 16.0 / 16.0 ** 0.5
    EPS = 1e-5
    WC = w_all.shape[1]
    VCUT = 18
    COLS = [(0, E), (E, 2 * E), (2 * E, 2 * E + VCUT * D), (2 * E + VCUT * D, WC)]
    MID = (H - VCUT) * D
    MASK_ID = 163.0
    MASK_TRI = MASK / SCALE / MASK_ID
    assert NT == 2 and WC == 3 * E + ER + NE and MASK_TRI == -1632.0

    ORDER = plan(NB, NU)
    place = {step: i for i, step in enumerate(ORDER)}
    nth, seen, misc_no, banked = {}, {}, {}, 0
    for step in ORDER:
        nth[step] = seen.get(step[0], 0)
        seen[step[0]] = nth[step] + 1
        first = step[0] not in ("proj", "wo") or step[-1] == 0
        if step[0] in ("xt", "proj", "qkt", "otok", "ctxt", "gmt", "delta", "wo", "mt") and first:
            misc_no[step] = banked
            banked += 1
        elif not first:
            misc_no[step] = misc_no[step[:-1] + (0,)]

    with ExitStack() as ctx:
        def sb(name, shape, dt=F32):
            return ctx.enter_context(nc.sbuf_tensor(name, shape, dt))

        def psum(name):
            return ctx.enter_context(nc.psum_tensor(name, [P, 512], F32))

        def sem(name):
            return ctx.enter_context(nc.semaphore(name))

        NX = 3
        xs = sb("xs", [P, NX, NT, E])
        xn = sb("xn", [P, NT, E])
        x_hi = sb("x_hi", [P, NT, KC, P], F32R)
        x_lo = sb("x_lo", [P, NT, KC, P], F32R)
        w_hi = sb("w_hi", [P, KC, WC], F32R)
        w_lo = sb("w_lo", [P, KC, WC], F32R)
        wo_hi = sb("wo_hi", [P, KC, E], F32R)
        wo_lo = sb("wo_lo", [P, KC, E], F32R)
        bias_rows = sb("bias_rows", [2, E + WC], F32R)
        ones_rows = sb("ones_rows", [2, P], F32R)
        ones_b = sb("ones_b", [3, S], BF16)
        expert_out = sb("expert_out", [ER, E])
        cos_t = sb("cos_t", [P, NT, D])
        sin_t = sb("sin_t", [P, NT, D])
        qk_rot = sb("qk_rot", [P, NT, 2, E])
        rope_sin_part = sb("rope_sin_part", [P, 2, E])
        parts = sb("parts", [P, 6, 4, S], BF16)
        part_rest = sb("part_rest", [P, E])
        stack = sb("stack", [P, 2, H, S], BF16)
        v_ones = sb("v_ones", [P, 2, NT, H, D + 1])
        probs = sb("probs", [P, 6, 512])
        o_t = sb("o_t", [P, NU, S])
        ctx_n = sb("ctx_n", [P, NT, E])
        ctx_hi = sb("ctx_hi", [P, KC, P], F32R)
        ctx_lo = sb("ctx_lo", [P, KC, P], F32R)
        fin = sb("fin", [P, 2, E])
        ident = sb("ident", [P, P])
        ident_b = sb("ident_b", [P, P], BF16)
        mask_id = sb("mask_id", [P, P], BF16)
        tri_row = sb("tri_row", [P, P], BF16)
        tri_col = sb("tri_col", [P, P], BF16)
        ln_st = sb("ln_st", [P, NT, 6])
        ln_mv = sb("ln_mv", [P, NT, 2])
        ln_ve = sb("ln_ve", [P, NT, 1])
        ln_rs = sb("ln_rs", [P, NT, 1])
        neg_half = sb("neg_half", [P, NT, 1])
        mx = sb("mx", [P, 2, NT, 8])
        m_parts = sb("m_parts", [P, 2, NT, 3, 8], BF16)
        m_rest = sb("m_rest", [P, NT, 8])
        m_rows = sb("m_rows", [24, 2, S], BF16)
        NMISC = 3
        rsum = sb("rsum", [P, NMISC, 16])
        ar = sb("ar", [P, 2, NT, ER + NE])
        before = sb("before", [P, NE, NE])
        g_gt = sb("g_gt", [P, NT, NE, NE])
        g_eq = sb("g_eq", [P, NT, NE, NE])
        g_rank = sb("g_rank", [P, NT, NE])
        g_max = sb("g_max", [P, NT, 1])
        g_exp = sb("g_exp", [P, NT, NE])
        g_sum = sb("g_sum", [P, NT, 1])
        gm = sb("gm", [P, NT, ER])
        gm_t = sb("gm_t", [ER, S])

        w_raw = stack[:, :, :, :].rearrange("p a h s -> p (a h s)").bitcast(F32)
        wo_raw = probs[:, :, :].rearrange("p a n -> p (a n)")[:, 0:KC * E].rearrange("p (k n) -> p k n", k=KC)
        BC = 4 * E // P
        bias_raw, bias_hi, bias_lo = o_t[:, 0, 0:BC], o_t[:, 0, BC:2 * BC], o_t[:, 0, 2 * BC:3 * BC]
        WP, at = [], 0
        for c0, c1 in ((0, E), (E, 2 * E), (2 * E, WC)):
            for k in range(0, KC, 2):
                raw = w_raw[:, at:at + 2 * (c1 - c0)].rearrange("p (k n) -> p k n", k=2)
                WP.append((raw, w_hi[:, k:k + 2, c0:c1], w_lo[:, k:k + 2, c0:c1], (c0, c1), k))
                at += 2 * (c1 - c0)
        for k in range(0, KC, 2):
            WP.append((wo_raw[:, k:k + 2, :], wo_hi[:, k:k + 2, :], wo_lo[:, k:k + 2, :], None, k))
        NWQ = len(WP) - 2

        row_bank = [psum("row_bank0"), psum("row_bank1")]
        t_bank = [psum("t_bank0"), psum("t_bank1")]
        o_bank = psum("o_bank")
        misc_bank = [psum(f"misc_bank{i}") for i in range(NMISC)]

        x_in = [sem(f"x_in{f}") for f in range(NT)] + [sem(f"x_in_row{b}") for b in range(1, NB)]
        w_in = [sem(f"w_in{i}") for i in range(len(WP))]
        bias_in, eb_in, rope_in = sem("bias_in"), sem("eb_in"), sem("rope_in")
        ident_ready, masks_ready, v_ones_ready = sem("ident_ready"), sem("masks_ready"), sem("v_ones_ready")
        stack_ones, ones_b_ready = sem("stack_ones"), sem("ones_b_ready")
        w_hi_done, w_lo_done = sem("w_hi_done"), sem("w_lo_done")
        bias_split, bias_rows_in, zeros_ready = sem("bias_split"), sem("bias_rows_in"), sem("zeros_ready")
        dve_step = sem("dve_step")
        pool_step = sem("pool_step")
        stats_ready, rstd_ready, xn_ready = sem("stats_ready"), sem("rstd_ready"), sem("xn_ready")
        xh_ready, ar_v_ready = sem("xh_ready"), sem("ar_v_ready")
        misc_full = [sem(f"misc_full{i}") for i in range(NMISC)]
        misc_free = [sem(f"misc_free{i}") for i in range(NMISC)]
        rope_done = sem("rope_done")
        qh_ready, parts_ready = sem("qh_ready"), sem("parts_ready")
        stack_in = [sem(f"stack_in{u}") for u in range(NU)]
        row_full, row_max = sem("row_full"), sem("row_max")
        mp_ready, m_copied = sem("mp_ready"), sem("m_copied")
        m_in = [sem("m_in0"), sem("m_in1")]
        t_full, exp_done = sem("t_full"), sem("exp_done")
        o_full, o_copied = sem("o_full"), sem("o_copied")
        o_zeroed = sem("o_zeroed")
        ch_ready = sem("ch_ready")
        gate_dl, gate_exp, gm_ready = sem("gate_dl"), sem("gate_exp"), sem("gm_ready")
        tanh_done, out_ready = sem("tanh_done"), sem("out_ready")
        stored = [sem("stored0"), sem("stored1")]

        def misc(step):
            return misc_bank[misc_no[step] % NMISC]

        def misc_freed(step):
            return misc_free[misc_no[step] % NMISC]

        def wait_misc_full(eng, step):
            eng.wait_ge(misc_full[misc_no[step] % NMISC], misc_no[step] // NMISC + 1)

        def wait_misc_free(eng, step):
            if misc_no[step] >= NMISC:
                eng.wait_ge(misc_freed(step), misc_no[step] // NMISC)

        def wait_misc_read(eng, step):
            eng.wait_ge(misc_freed(step), misc_no[step] // NMISC + 1)

        rope_no = {step: i for i, step in enumerate(s for s in ORDER if s[0] == "proj" and s[3] < 2 and s[4] == KC - 1)}

        block = ctx.enter_context(nc.Block())

        @block.sync
        def _(sp):
            x_v = x.rearrange("b (t p) e -> b p t e", p=P)
            w_v = w_all.rearrange("(k p) n -> p k n", p=P)
            for t in range(NT):
                sp.dma_start(xs[:, 0, t, :], x_v[0, :, t, :]).then_inc(x_in[t], 16)
            for i, (raw, _, _, cols, k) in enumerate(WP):
                source = w_out.rearrange("(k p) n -> p k n", p=P) if cols is None else w_v[:, :, cols[0]:cols[1]]
                if i == NWQ:
                    sp.dma_start(xs[:, 1, :, :], x_v[1]).then_inc(x_in[NT], 16)
                sp.dma_start(raw, source[:, k:k + 2, :]).then_inc(w_in[i], 16)
                if i == 1:
                    sp.dma_start(cos_t[:, :, :], rope_cos.rearrange("(t p) d -> p t d", p=P)).then_inc(rope_in, 16)
                    sp.dma_start(sin_t[:, :, :], rope_sin.rearrange("(t p) d -> p t d", p=P)).then_inc(rope_in, 16)
            sp.dma_start(xs[:, 2, :, :], x_v[2]).then_inc(x_in[NT + 1], 16)
            sp.dma_start(expert_out[:, :], experts_b).then_inc(eb_in, 16)
            sp.wait_ge(w_lo_done, NWQ)
            sp.wait_ge(ones_b_ready, 1)
            sp.dma_start(stack[96:99, 1, :, :], ones_b[:, :].unsqueeze(1).broadcast_to([3, H, S])).then_inc(stack_ones, 16)

            for step in ORDER:
                kind = step[0]
                if kind == "stack":
                    _, b, u = step
                    sp.wait_ge(parts_ready, 4 * (b + 1))
                    if b:
                        sp.wait_ge(t_full, 3 * (NU * (b - 1) + u + 1))
                    for slot, (qp, kp) in enumerate(((0, 0), (0, 1), (0, 2), (1, 0), (1, 1), (2, 0))):
                        sp.dma_start(stack[D * slot:D * (slot + 1), :, 4 * u:4 * u + 4, :],
                                     parts[D * u:D * (u + 1), qp:4 + kp:3 + kp - qp, :, :]).then_inc(stack_in[u], 16)
                if kind == "wo" and step[3] == KC - 1:
                    _, b, t, k = step
                    f = NT * b + t
                    sp.wait_ge(out_ready, f + 1)
                    sp.dma_start(out[b, t * P:(t + 1) * P, :], fin[:, f % 2, :]).then_inc(stored[f % 2], 16)
                    if t == NT - 1 and b + NX < NB:
                        sp.dma_start(xs[:, b % NX, :, :], x_v[b + NX]).then_inc(x_in[NT + b + NX - 1], 16)
            for q in stored:
                sp.wait_ge(q, 16 * (NB * NT // 2))

        @block.gpsimd
        def _(pool):
            n = [0]

            def link(ins):
                n[0] += 1
                ins.then_inc(pool_step, 1)
                pool.wait_ge(pool_step, n[0])

            def masked(tile, value, op, step, mult):
                link(pool.memset(tile[:, :], value))
                return pool.affine_select(out=tile[:, :], in_=tile[:, :], compare_op=op, fill=0.0, base=0,
                                          pattern=[[step, tile.shape[1]]], channel_multiplier=mult)

            link(pool.memset(neg_half[:, :, :], -0.5))
            masked(ident, 1.0, ALU.is_equal, -1, 1).then_inc(ident_ready, 1)
            pool.memset(ones_rows[:, :].bitcast(F32), 1.0).then_inc(zeros_ready, 1)
            masked(ident_b, 1.0, ALU.is_equal, -1, 1).then_inc(masks_ready, 1)
            masked(mask_id, MASK_ID, ALU.is_equal, -1, 1).then_inc(masks_ready, 1)
            masked(tri_row, MASK_TRI, ALU.is_gt, -1, 1).then_inc(masks_ready, 1)
            masked(tri_col, MASK_TRI, ALU.is_gt, 1, -1).then_inc(masks_ready, 1)
            pool.memset(ones_b[:, :], 1.0).then_inc(ones_b_ready, 1)
            pool.memset(v_ones[:, :, :, :, D:D + 1].rearrange("p a t h d -> p (a t h) d"), 1.0).then_inc(v_ones_ready, 1)

            for step in ORDER:
                kind = step[0]
                if kind == "ln_stats":
                    _, b, t = step
                    pool.wait_ge(stats_ready, nth[step] + 1)
                    link(pool.tensor_scalar(ln_ve[:, t, :], ln_mv[:, t, 1:2], EPS, None, ALU.add))
                    pool.tensor_tensor(ln_rs[:, t, :], ln_ve[:, t, :], neg_half[:, t, :], ALU.pow).then_inc(rstd_ready, 1)
                if kind == "proj" and step[3] < 2 and step[4] == KC - 1:
                    _, b, t, w, k = step
                    r = rope_no[step]
                    wait_misc_read(pool, step)
                    pool.tensor_tensor(qk_rot[:, t, w, :], qk_rot[:, t, w, :], rope_sin_part[:, r % 2, :],
                                       ALU.add).then_inc(rope_done, 1)
                if kind == "wo" and step[3] == KC - 1:
                    _, b, t, k = step
                    f = NT * b + t
                    wait_misc_read(pool, step)
                    pool.tensor_tensor(fin[:, f % 2, :], fin[:, f % 2, :], xs[:, b % NX, t, :],
                                       ALU.add).then_inc(out_ready, 1)

        @block.scalar
        def _(act):
            act.dma_start(bias_raw, bias.rearrange("o (p j) -> (o p) j", p=P)).then_inc(bias_in, 16)
            for step in ORDER:
                kind = step[0]
                if kind == "bias":
                    act.wait_ge(bias_split, 1)
                    for row, part in enumerate((bias_hi, bias_lo)):
                        act.dma_start(bias_rows[row:row + 1, 0:4 * E].bitcast(F32), part).then_inc(bias_rows_in, 16)
                if kind == "weights":
                    raw, hi, lo, _, _ = WP[step[2]]
                    act.wait_ge(w_in[step[2]], 16)
                    nc.scalar.activation(hi, raw, ACT.Copy).then_inc(w_hi_done, 1)
                if kind == "xt":
                    _, b, t = step
                    wait_misc_full(act, step)
                    if b:
                        wait_misc_full(act, max((("proj", b - 1, t, c, KC - 1) for c in range(4)), key=place.get))
                    nc.scalar.activation(x_hi[:, t, :, :], misc(step)[:, :].rearrange("p (k n) -> p k n", k=KC),
                                         ACT.Copy).then_inc(xh_ready, 1)
                if kind == "qkt":
                    _, b, t, w = step
                    wait_misc_full(act, step)
                    if b and nth[step] % 4 == 0:
                        for u in range(NU):
                            act.wait_ge(stack_in[u], 96 * b)
                    nc.scalar.activation(parts[:, 3 * w, :, t * P:(t + 1) * P],
                                         misc(step)[:, :].rearrange("p (g n) -> p g n", g=4),
                                         ACT.Copy).then_inc(qh_ready, 1)
                if kind == "proj" and step[3] >= 2 and step[4] == KC - 1:
                    _, b, t, c, k = step
                    wait_misc_full(act, step)
                    if b >= 2:
                        act.wait_ge(o_full, NU * (b - 1))
                    elif b == 0:
                        act.wait_ge(v_ones_ready, 1)
                    h0, h1 = (0, VCUT) if c == 2 else (VCUT, H)
                    cols = (h1 - h0) * D
                    if c == 3:
                        nc.scalar.activation(ar[:, b % 2, t, :], misc(step)[:, cols:cols + ER + NE],
                                             ACT.Copy).then_inc(ar_v_ready, 1)
                    nc.scalar.activation(v_ones[:, b % 2, t, h0:h1, 0:D],
                                         misc(step)[:, 0:cols].rearrange("p (h d) -> p h d", d=D),
                                         ACT.Copy).then_inc(misc_freed(step), 1)
                if kind == "mt":
                    s = step[1]
                    b, g = s // NG, s % NG
                    wait_misc_full(act, step)
                    if s >= 2:
                        act.wait_ge(m_in[s % 2], 16 * (s // 2))
                    nc.scalar.activation(m_rows[:, s % 2, :], misc(step)[0:24, 0:P].bitcast(BF16),
                                         ACT.Copy).then_inc(misc_freed(step), 1)
                    wait_misc_read(act, step)
                    if b:
                        act.wait_ge(t_full, 3 * (NU * (b - 1) + 2 * g + 2))
                    act.dma_start(stack[96:99, 0, 8 * g:8 * g + 8, :], m_rows[:, s % 2, :]).then_inc(m_in[s % 2], 16)
                if kind == "tt":
                    n = step[1]
                    U = n // 3
                    act.wait_ge(t_full, n + 1)
                    if U >= 2 and n % 3 == 0:
                        act.wait_ge(o_full, U - 1)
                    if n == 0:
                        act.wait_ge(w_lo_done, len(WP))
                    nc.scalar.activation(probs[:, n % 6, :], t_bank[n % 2][:, :], ACT.Exp,
                                         scale=SCALE).then_inc(exp_done, 1)
                if kind == "ov":
                    U = step[1]
                    b, u = U // NU, U % NU
                    act.wait_ge(o_full, U + 1)
                    if b:
                        wait_misc_full(act, ("otok", b - 1, u // 4, 1))
                    elif u == 0:
                        act.wait_ge(bias_rows_in, 32)
                    nc.scalar.activation(o_t[:, u, :], o_bank[:, 0:S], ACT.Copy).then_inc(o_copied, 1)
                if kind == "ctxt":
                    _, b, t = step
                    wait_misc_full(act, step)
                    f = NT * b + t
                    if f:
                        wait_misc_full(act, ("wo", (f - 1) // NT, (f - 1) % NT, 0))
                    nc.scalar.activation(ctx_hi[:, :, :], misc(step)[:, :].rearrange("p (k n) -> p k n", k=KC),
                                         ACT.Copy).then_inc(ch_ready, 1)
                if kind == "gate_a":
                    b = step[1]
                    act.wait_ge(gate_dl, b + 1)
                    nc.scalar.activation(g_exp[:, :, :], g_exp[:, :, :], ACT.Exp).then_inc(gate_exp, 1)
                if kind == "delta":
                    _, b, t = step
                    f = NT * b + t
                    wait_misc_full(act, step)
                    if f >= 2:
                        act.wait_ge(stored[f % 2], 16 * (f // 2))
                    nc.scalar.activation(fin[:, f % 2, :], misc(step)[:, :], ACT.Tanh,
                                         scale=0.5).then_inc(tanh_done, 1)

        @block.vector
        def _(dve):
            n = [0]

            def link(ins):
                n[0] += 1
                ins.then_inc(dve_step, 1)
                dve.wait_ge(dve_step, n[0])

            link(dve.memset(before[:, :, :], 0.0))
            for e in range(1, NE):
                last = dve.memset(before[:, e, 0:e], 1.0)
            link(last)
            dve.memset(bias_rows[:, 4 * E:E + WC].bitcast(F32), 0.0).then_inc(zeros_ready, 1)
            dve.memset(o_bank[:, 0:S], 0.0).then_inc(o_zeroed, 1)

            for step in ORDER:
                kind = step[0]
                if kind == "bias":
                    dve.wait_ge(bias_in, 16)
                    link(dve.tensor_copy(bias_hi.bitcast(F32R), bias_raw))
                    dve.tensor_tensor(bias_lo.bitcast(F32R), bias_raw, bias_hi, ALU.subtract).then_inc(bias_split, 1)
                if kind == "weights":
                    i = step[2]
                    raw, hi, lo, _, _ = WP[i]
                    dve.wait_ge(w_hi_done, i + 1)
                    dve.tensor_tensor(lo, raw, hi.bitcast(F32), ALU.subtract).then_inc(w_lo_done, 1)
                if kind == "ln_stats":
                    _, b, t = step
                    dve.wait_ge(x_in[b + NT - 1] if b else x_in[t], 16)
                    link(dve.bn_stats(ln_st[:, t, :], xs[:, b % NX, t, :]))
                    dve.bn_aggr(ln_mv[:, t, :], ln_st[:, t, :]).then_inc(stats_ready, 1)
                if kind == "ln_apply":
                    _, b, t = step
                    dve.wait_ge(rstd_ready, nth[step] + 1)
                    dve.tensor_scalar(xn[:, t, :], xs[:, b % NX, t, :], ln_mv[:, t, 0:1], ln_rs[:, t, 0:1],
                                      ALU.subtract, ALU.mult).then_inc(xn_ready, 1)
                if kind == "xt":
                    _, b, t = step
                    dve.wait_ge(xh_ready, nth[step] + 1)
                    dve.tensor_tensor(x_lo[:, t, :, :], misc(step)[:, :].rearrange("p (k n) -> p k n", k=KC),
                                      x_hi[:, t, :, :].bitcast(F32), ALU.subtract).then_inc(misc_freed(step), 1)
                if kind == "proj" and step[3] < 2 and step[4] == KC - 1:
                    _, b, t, w, k = step
                    r = rope_no[step]
                    wait_misc_full(dve, step)
                    if r == 0:
                        dve.wait_ge(rope_in, 32)
                    if r >= 2:
                        dve.wait_ge(rope_done, r - 1)
                    q = misc(step)[:, :].rearrange("p (h d) -> p h d", d=D)
                    dve.tensor_tensor(qk_rot[:, t, w, :].rearrange("p (h d) -> p h d", d=D), q,
                                      cos_t[:, t:t + 1, :].broadcast_to([P, H, D]), ALU.mult)
                    dve.tensor_tensor(
                        rope_sin_part[:, r % 2, :].rearrange("p (h a d) -> p h a d", a=2, d=HALF),
                        misc(step)[:, :].rearrange("p (h a d) -> p h a d", a=2, d=HALF)[:, :, ::-1, :],
                        sin_t[:, t, :].rearrange("p (a d) -> p a d", a=2).unsqueeze(1).broadcast_to([P, H, 2, HALF]),
                        ALU.mult).then_inc(misc_freed(step), 1)
                if kind == "qkt":
                    _, b, t, w = step
                    r = nth[step]
                    dve.wait_ge(qh_ready, r + 1)
                    if r:
                        dve.wait_ge(parts_ready, r)
                    rest = part_rest[:, :].rearrange("p (g n) -> p g n", g=4)
                    pw = parts[:, 3 * w:3 * w + 3, :, t * P:(t + 1) * P]
                    dve.tensor_tensor(rest, misc(step)[:, :].rearrange("p (g n) -> p g n", g=4), pw[:, 0, :, :],
                                      ALU.subtract).then_inc(misc_freed(step), 1)
                    wait_misc_read(dve, step)
                    link(dve.tensor_copy(pw[:, 1, :, :], rest))
                    dve.tensor_tensor(pw[:, 2, :, :], rest, pw[:, 1, :, :], ALU.subtract).then_inc(parts_ready, 1)
                if kind == "row":
                    n_ = step[1]
                    U, i = n_ // 3, n_ % 3
                    m, o = mx[:, U // 2 % 2, :, :], 4 * (U % 2)
                    t, h0, h1 = (0, o, o + 4) if i == 0 else (1, o + 2 * i - 2, o + 2 * i)
                    dve.wait_ge(row_full, n_ + 1)
                    dve.tensor_reduce(m[:, t, h0:h1], row_bank[n_ % 2][:, :].rearrange("p (h n) -> p h n", h=h1 - h0),
                                      AX.X, ALU.max).then_inc(row_max, 1)
                if kind == "msplit":
                    s = step[1]
                    dve.wait_ge(row_max, 6 * (s + 1))
                    if s >= 2:
                        wait_misc_full(dve, ("mt", s - 2))
                    m, mp = mx[:, s % 2, :, :], m_parts[:, s % 2, :, :, :]
                    link(dve.tensor_scalar(mp[:, :, 0, :], m, -1.0, None, ALU.mult))
                    link(dve.scalar_tensor_tensor(m_rest[:, :, :], m, -1.0, mp[:, :, 0, :], ALU.mult, ALU.subtract))
                    link(dve.tensor_copy(mp[:, :, 1, :], m_rest[:, :, :]))
                    dve.tensor_tensor(mp[:, :, 2, :], m_rest[:, :, :], mp[:, :, 1, :],
                                      ALU.subtract).then_inc(mp_ready, 1)
                if kind == "otok":
                    _, b, half, t = step
                    wait_misc_full(dve, step)
                    o = misc(step)[:, :].rearrange("p (h d) -> p h d", d=2 * D)
                    link(dve.reciprocal(rsum[:, misc_no[step] % NMISC, :].rearrange("p (h d) -> p h d", d=1), o[:, :, D:D + 1]))
                    dve.tensor_tensor(
                        ctx_n[:, t, half * 256:(half + 1) * 256].rearrange("p (h d) -> p h d", d=D), o[:, :, 0:D],
                        rsum[:, misc_no[step] % NMISC, :].rearrange("p (h d) -> p h d", d=1).broadcast_to([P, 16, D]),
                        ALU.mult).then_inc(misc_freed(step), 1)
                if kind == "ctxt":
                    _, b, t = step
                    dve.wait_ge(ch_ready, nth[step] + 1)
                    dve.tensor_tensor(ctx_lo[:, :, :], misc(step)[:, :].rearrange("p (k n) -> p k n", k=KC),
                                      ctx_hi[:, :, :].bitcast(F32), ALU.subtract).then_inc(misc_freed(step), 1)
                if kind == "gate_a":
                    b = step[1]
                    dve.wait_ge(ar_v_ready, NT * (b + 1))
                    lg = ar[:, b % 2, :, ER:ER + NE]
                    for t in range(NT):
                        of_j = lg[:, t:t + 1, :].broadcast_to([P, NE, NE])
                        of_e = lg[:, t, :].unsqueeze(2).broadcast_to([P, NE, NE])
                        dve.tensor_tensor(g_gt[:, t, :, :], of_j, of_e, ALU.is_gt)
                        last = dve.tensor_tensor(g_eq[:, t, :, :], of_j, of_e, ALU.is_equal)
                    link(last)
                    for t in range(NT):
                        last = dve.tensor_tensor(g_eq[:, t, :, :], g_eq[:, t, :, :], before[:, :, :], ALU.mult)
                    link(last)
                    link(dve.tensor_tensor(g_gt[:, :, :, :], g_gt[:, :, :, :], g_eq[:, :, :, :], ALU.add))
                    dve.tensor_reduce(g_rank[:, :, :], g_gt[:, :, :, :], AX.X, ALU.add)
                    link(dve.tensor_reduce(g_max[:, :, :], lg, AX.X, ALU.max))
                    dve.tensor_tensor(g_exp[:, :, :], lg, g_max[:, :, :].broadcast_to([P, NT, NE]),
                                      ALU.subtract).then_inc(gate_dl, 1)
                if kind == "gate_b":
                    b = step[1]
                    dve.wait_ge(gate_exp, b + 1)
                    link(dve.scalar_tensor_tensor(g_exp[:, :, :], g_rank[:, :, :], 2.0, g_exp[:, :, :], ALU.is_lt,
                                                  ALU.mult))
                    link(dve.tensor_reduce(g_sum[:, :, :], g_exp[:, :, :], AX.X, ALU.add))
                    link(dve.reciprocal(g_sum[:, :, :], g_sum[:, :, :]))
                    link(dve.scalar_tensor_tensor(g_exp[:, :, :], g_exp[:, :, :], LORA_SCALE,
                                                  g_sum[:, :, :].broadcast_to([P, NT, NE]), ALU.mult, ALU.mult))
                    for t in range(NT):
                        last = dve.tensor_tensor(gm[:, t, :].rearrange("p (e r) -> p e r", r=R),
                                                 ar[:, b % 2, t, 0:ER].rearrange("p (e r) -> p e r", r=R),
                                                 g_exp[:, t, :].unsqueeze(2).broadcast_to([P, NE, R]), ALU.mult)
                    last.then_inc(gm_ready, 1)
                if kind == "gmt":
                    wait_misc_full(dve, step)
                    dve.tensor_copy(gm_t[:, :], misc(step)[0:ER, 0:S]).then_inc(misc_freed(step), 1)
                if kind == "delta":
                    _, b, t = step
                    f = NT * b + t
                    dve.wait_ge(tanh_done, f + 1)
                    dve.scalar_tensor_tensor(fin[:, f % 2, :], fin[:, f % 2, :], 1.0, misc(step)[:, :], ALU.add,
                                             ALU.mult).then_inc(misc_freed(step), 1)
                if kind == "wo" and step[3] == KC - 1:
                    _, b, t, k = step
                    f = NT * b + t
                    wait_misc_full(dve, step)
                    wait_misc_read(dve, ("delta", b, t))
                    dve.scalar_tensor_tensor(fin[:, f % 2, :], fin[:, f % 2, :], 0.5, misc(step)[:, :], ALU.mult,
                                             ALU.mult).then_inc(misc_freed(step), 1)

        @block.tensor
        def _(pe):
            def three_passes(step, k, cols, hi, lo, rhs_hi, rhs_lo, bias_at):
                bank = misc(step)[:, 0:cols]
                pe.matmul(bank, hi, rhs_hi, start=(k == 0), stop=False)
                pe.matmul(bank, hi, rhs_lo, start=False, stop=False)
                last = pe.matmul(bank, lo, rhs_hi, start=False, stop=False)
                if k == KC - 1:
                    if nth[step] == KC - 1 and step[0] == "proj":
                        pe.wait_ge(zeros_ready, 2)
                        pe.wait_ge(bias_rows_in, 32)
                    last = pe.matmul(bank, ones_rows[:, :], bias_rows[:, bias_at:bias_at + cols], start=False,
                                     stop=True)
                    last.then_inc(misc_full[misc_no[step] % NMISC], 1)

            for step in ORDER:
                kind = step[0]
                if step in misc_no and (kind not in ("proj", "wo") or step[-1] == 0):
                    wait_misc_free(pe, step)
                if kind == "xt":
                    _, b, t = step
                    if b == 0 and t == 0:
                        pe.wait_ge(ident_ready, 1)
                    pe.wait_ge(xn_ready, nth[step] + 1)
                    for k in range(KC):
                        last = pe.transpose(misc(step)[:, k * P:(k + 1) * P], xn[:, t, k * P:(k + 1) * P], ident[:, :])
                    last.then_inc(misc_full[misc_no[step] % NMISC], 1)
                if kind == "proj":
                    _, b, t, c, k = step
                    if k == 0:
                        wait_misc_read(pe, ("xt", b, t))
                    if b == 0 and k % 2 == 0:
                        pe.wait_ge(w_lo_done, 2 * min(c, 2) + k // 2 + 1)
                    c0, c1 = COLS[c]
                    three_passes(step, k, c1 - c0, x_hi[:, t, k, :], x_lo[:, t, k, :], w_hi[:, k, c0:c1],
                                 w_lo[:, k, c0:c1], E + c0)
                if kind == "qkt":
                    _, b, t, w = step
                    pe.wait_ge(rope_done, rope_no[("proj", b, t, w, KC - 1)] + 1)
                    for g in range(4):
                        last = pe.transpose(misc(step)[:, g * P:(g + 1) * P], qk_rot[:, t, w, g * P:(g + 1) * P],
                                            ident[:, :])
                    last.then_inc(misc_full[misc_no[step] % NMISC], 1)
                if kind == "row":
                    n = step[1]
                    U, i = n // 3, n % 3
                    b, u = U // NU, U % NU
                    pe.wait_ge(stack_in[u], 96 * (b + 1))
                    if n == 0:
                        pe.wait_ge(masks_ready, 4)
                    if n >= 2:
                        pe.wait_ge(row_max, n - 1)
                    heads = range(4) if i == 0 else range(2 * i - 2, 2 * i)
                    t = 0 if i == 0 else 1
                    bank = row_bank[n % 2][:, :].rearrange("p (h n) -> p h n", h=len(heads))
                    width = 512 // len(heads)
                    pe.matmul(bank[:, :, t * P:(t + 1) * P], tri_row[:, :],
                              mask_id[:, :].unsqueeze(1).broadcast_to([P, len(heads), P]), start=True, stop=False,
                              skip_group_check=True)
                    for j, h in enumerate(heads):
                        last = pe.matmul(bank[:, j, :], stack[0:96, 0, 4 * u + h, t * P:(t + 1) * P],
                                         stack[0:96, 1, 4 * u + h, 0:width], start=False, stop=True,
                                         skip_group_check=True)
                    last.then_inc(row_full, 1)
                if kind == "mt":
                    s = step[1]
                    pe.wait_ge(mp_ready, s + 1)
                    for t in range(NT):
                        last = pe.transpose(misc(step)[0:24, t * 64:(t + 1) * 64].bitcast(BF16),
                                            m_parts[:, s % 2, t, :, :].rearrange("p a h -> p (a h)"), ident_b[:, :])
                    last.then_inc(misc_full[misc_no[step] % NMISC], 1)
                if kind == "tt":
                    n = step[1]
                    U, i = n // 3, n % 3
                    b, u, s = U // NU, U % NU, U // 2
                    pe.wait_ge(m_in[s % 2], 16 * (s // 2 + 1))
                    if n == 0:
                        pe.wait_ge(stack_ones, 16)
                    if n >= 2:
                        pe.wait_ge(exp_done, n - 1)
                    heads = range(4) if i == 2 else range(2 * i, 2 * i + 2)
                    kb, q0 = (1, P) if i == 2 else (0, 0)
                    bank = t_bank[n % 2][:, :].rearrange("p (h n) -> p h n", h=len(heads))
                    pe.matmul(bank[:, :, 0:P], tri_col[:, :],
                              mask_id[:, :].unsqueeze(1).broadcast_to([P, len(heads), P]), start=True, stop=False,
                              skip_group_check=True)
                    for j, h in enumerate(heads):
                        last = pe.matmul(bank[:, j, :], stack[0:99, 1, 4 * u + h, kb * P:(kb + 1) * P],
                                         stack[0:99, 0, 4 * u + h, q0:S], start=False, stop=True,
                                         skip_group_check=True)
                    last.then_inc(t_full, 1)
                if kind == "pv":
                    U = step[1]
                    b, u = U // NU, U % NU
                    pe.wait_ge(exp_done, 3 * U + 3)
                    if u == 0:
                        for t in range(NT):
                            for c in (2, 3):
                                wait_misc_read(pe, ("proj", b, t, c, KC - 1))
                    if U == 0:
                        pe.wait_ge(o_zeroed, 1)
                    else:
                        pe.wait_ge(o_copied, U)
                    for kb in range(2):
                        for h in range(4):
                            n = 3 * U + (2 if kb else h // 2)
                            width = S - kb * P
                            at = h * width if kb else (h % 2) * width
                            last = pe.matmul(o_bank[32 * h:32 * h + D + 1, kb * P:S], v_ones[:, b % 2, kb, 8 * h + u, :],
                                             probs[:, n % 6, at:at + width], start=(kb == 0), stop=(kb == 1),
                                             skip_group_check=True)
                    last.then_inc(o_full, 1)
                if kind == "otok":
                    _, b, half, t = step
                    pe.wait_ge(o_copied, NU * b + 4 * half + 4)
                    for j in range(4):
                        last = pe.transpose(misc(step)[:, j * P:(j + 1) * P],
                                            o_t[:, 4 * half + j, t * P:(t + 1) * P], ident[:, :])
                    last.then_inc(misc_full[misc_no[step] % NMISC], 1)
                if kind == "ctxt":
                    _, b, t = step
                    for half in range(2):
                        wait_misc_read(pe, ("otok", b, half, t))
                    for k in range(KC):
                        last = pe.transpose(misc(step)[:, k * P:(k + 1) * P], ctx_n[:, t, k * P:(k + 1) * P],
                                            ident[:, :])
                    last.then_inc(misc_full[misc_no[step] % NMISC], 1)
                if kind == "gmt":
                    b = step[1]
                    pe.wait_ge(gm_ready, b + 1)
                    for t in range(NT):
                        last = pe.transpose(misc(step)[0:ER, t * P:(t + 1) * P], gm[:, t, :], ident[:, :])
                    last.then_inc(misc_full[misc_no[step] % NMISC], 1)
                if kind == "delta":
                    _, b, t = step
                    wait_misc_read(pe, ("gmt", b))
                    if b == 0:
                        pe.wait_ge(eb_in, 16)
                    pe.matmul(misc(step)[:, :], gm_t[:, t * P:(t + 1) * P], expert_out[:, :], start=True,
                              stop=True).then_inc(misc_full[misc_no[step] % NMISC], 1)
                if kind == "wo":
                    _, b, t, k = step
                    wait_misc_read(pe, ("ctxt", b, t))
                    if b == 0:
                        pe.wait_ge(w_lo_done, len(WP))
                    three_passes(step, k, E, ctx_hi[:, k, :], ctx_lo[:, k, :], wo_hi[:, k, :], wo_lo[:, k, :], 0)


def kernel(L0_attn_hidden_states, L0_attn_qkv_w, L0_attn_qkv_b, L0_attn_out_w, L0_attn_out_b, L0_ffn_router_w,
           L0_ffn_A, L0_ffn_B):
    import numpy as np
    import concourse.bacc as bacc
    from concourse.bass_utils import run_bass_kernel_spmd

    x = np.ascontiguousarray(L0_attn_hidden_states)
    NB, S, E = x.shape
    H, D = 32, 16
    w_all = np.concatenate([L0_attn_qkv_w, np.transpose(L0_ffn_A.reshape(-1, E)), np.transpose(L0_ffn_router_w)], axis=1)
    bias = np.concatenate([L0_attn_out_b, L0_attn_qkv_b])[None, :]
    w_out = L0_attn_out_w.reshape(4, 8, D, E).transpose(1, 0, 2, 3).reshape(E, E)
    experts_b = np.transpose(L0_ffn_B, (0, 2, 1)).reshape(-1, E)
    half = D // 2
    inv_freq = (1.0 / np.float32(10000.0) ** (np.arange(half, dtype=np.float32) / np.float32(half))).astype(np.float32)
    ang = np.arange(S, dtype=np.float32)[:, None] * inv_freq[None, :]
    cos, sin = np.cos(ang).astype(np.float32), np.sin(ang).astype(np.float32)
    arrays = {
        "in_x": x, "in_w_all": w_all, "in_bias": bias, "in_w_out": w_out, "in_experts_b": experts_b,
        "in_rope_cos": np.concatenate([cos, cos], axis=1), "in_rope_sin": np.concatenate([-sin, sin], axis=1),
    }
    arrays = {k: np.ascontiguousarray(v) for k, v in arrays.items()}
    nc = bacc.Bacc("TRN2", target_bir_lowering=False, num_devices=1)
    args = [nc.dram_tensor(k, v.shape, mybir.dt.from_np(v.dtype), kind="ExternalInput").ap() for k, v in arrays.items()]
    out = nc.dram_tensor("out_0", x.shape, F32, kind="ExternalOutput").ap()
    bass_attention_times_silu_lora(nc, *args, out)
    r = run_bass_kernel_spmd(nc, [arrays], core_ids=[0])
    return r.results[0]["out_0"]
```

```python
from contextlib import ExitStack

import concourse.bass as bass
from concourse import mybir
from concourse.alu_op_type import AluOpType as ALU

F32 = mybir.dt.float32
F32R = mybir.dt.float32r
BF16 = mybir.dt.bfloat16
ACT = mybir.ActivationFunctionType
AX = mybir.AxisListType

P = 128
MASK = -66504.0


ATTENTION = {
    ("row", 0): -10, ("row", 1): -4, ("row", 2): 17, ("row", 3): 32, ("row", 4): 40, ("row", 5): 58,
    ("msplit",): 63, ("mt",): 89, ("tt", 0): 123, ("tt", 1): 134, ("tt", 2): 140, ("tt", 3): 165,
    ("pv", 0): 171, ("ov", 0): 174, ("tt", 4): 174, ("tt", 5): 174, ("pv", 1): 204, ("ov", 1): 206,
}
ROW = {
    ("ln_stats", 0): -454, ("ln_stats", 1): -418, ("ln_apply", 0): -408, ("ln_apply", 1): -378, ("xt", 0): -377,
    ("xt", 1): -366, ("proj", 0, 0): (-359, 1), ("proj", 1, 0): (-358, 5), ("proj", 0, 1): (-326, 4),
    ("proj", 1, 1): (-313, 3), ("qkt", 1, 0): -283, ("qkt", 0, 0): -268, ("qkt", 1, 1): -249,
    ("proj", 0, 2): (-245, 1), ("qkt", 0, 1): -226, ("proj", 0, 3): (-218, 2), ("stack", 1): -193,
    ("stack", 0): -172, ("stack", 4): -159, ("stack", 2): -63, ("stack", 3): -59, ("proj", 1, 3): (-58, 4),
    ("proj", 1, 2): (-50, 4), ("stack", 5): -27, ("stack", 6): 7, ("stack", 7): 10, ("gate_a",): 327,
    ("gate_b",): 338, ("gmt",): 382, ("otok", 0, 0): 439, ("otok", 0, 1): 559, ("otok", 1, 0): 592,
    ("otok", 1, 1): 604, ("delta", 0): 614, ("ctxt", 0, 0): 634, ("ctxt", 0, 1): 635, ("delta", 1): 636,
    ("wo", 0): (667, 8), ("ctxt", 1, 0): 696, ("ctxt", 1, 1): 739, ("wo", 1): (797, 2),
}
FIRST = {
    ("bias",): -1180, ("ln_stats", 0): -1143, ("ln_apply", 0): -1142, ("ln_stats", 1): -1139,
    ("weights", 0): -1139, ("ln_apply", 1): -1138, ("xt", 0): -1131, ("weights", 1): -1131, ("xt", 1): -1104,
    ("weights", 2): -1037, ("weights", 3): -1017, ("weights", 4): -979, ("proj", 0, 0): (-968, 10),
    ("proj", 1, 0): (-926, 5), ("proj", 0, 1): (-894, 4), ("qkt", 0, 0): -884, ("proj", 1, 1): (-871, 2),
    ("qkt", 1, 0): -864, ("weights", 5): -862, ("qkt", 0, 1): -856, ("qkt", 1, 1): -838, ("stack", 0): -837,
    ("stack", 1): -835, ("stack", 2): -834, ("stack", 4): -834, ("proj", 0, 2): (-831, 14), ("stack", 5): -831,
    ("stack", 6): -830, ("stack", 3): -830, ("stack", 7): -829, ("proj", 1, 2): (-771, 1),
    ("proj", 1, 3): (-739, 1), ("proj", 0, 3): (-728, 1), ("weights", 6): -17, ("experts",): -10,
    ("weights", 7): 94,
}
SECOND = {
    ("ln_stats", 0): -1285, ("ln_apply", 0): -1227, ("ln_stats", 1): -1222, ("ln_apply", 1): -1221,
    ("xt", 0): -1082, ("xt", 1): -1068, ("proj", 0, 0): (-1062, 3), ("proj", 1, 0): (-409, 11),
    ("proj", 0, 1): (-408, 2), ("proj", 1, 1): (-355, 2), ("proj", 0, 2): (-331, 9), ("proj", 1, 2): (-281, 4),
    ("proj", 0, 3): (-255, 5), ("qkt", 1, 1): -224, ("proj", 1, 3): (-224, 5), ("qkt", 1, 0): -217,
    ("qkt", 0, 0): -205, ("qkt", 0, 1): -204,
}
LAST = {
    ("gate_a",): 124, ("gate_b",): 179, ("otok", 0, 0): 375, ("gmt",): 432, ("otok", 0, 1): 470,
    ("delta", 0): 476, ("delta", 1): 501, ("ctxt", 0, 0): 517, ("otok", 1, 0): 522, ("ctxt", 1, 0): 566,
    ("otok", 1, 1): 616, ("ctxt", 0, 1): 618, ("wo", 0): (625, 625, 625, 652), ("ctxt", 1, 1): 639,
    ("wo", 1): (810, 817, 822, 831),
}


def plan(NB, NU):
    NG = NU // 2
    at = {}
    for s in range(NB * NG):
        for name, tick in ATTENTION.items():
            kind, i = name[0], name[1:]
            if kind in ("row", "tt"):
                step = (kind, 6 * s + i[0])
            elif kind in ("pv", "ov"):
                step = (kind, 2 * s + i[0])
            else:
                step = (kind, s)
            at[step] = 100 * s + tick
    for b in range(NB):
        ticks = dict(ROW)
        if b == 0:
            ticks.update(FIRST)
        if b == 1:
            ticks.update(SECOND)
        if b == NB - 1:
            ticks.update(LAST)
        for name, tick in ticks.items():
            step = name[:1] + (b,) + name[1:]
            if name[0] in ("proj", "wo"):
                parts = tick if len(tick) == 4 else [tick[0] + tick[1] * k for k in range(4)]
                for k in range(4):
                    at[step + (k,)] = 100 * NG * b + parts[k]
            else:
                at[step] = 100 * NG * b + tick
    return sorted(at, key=at.get)


def bass_attention_times_silu_lora(nc, x, w_all, bias, w_out, experts_b, rope, out):
    NB, S, E = x.shape
    H, D = 32, 16
    HALF = D // 2
    NE, R = 4, 16
    ER = NE * R
    NT = S // P
    KC = E // P
    NU = H // 4
    NG = NU // 2
    SCALE = 1.0 / D ** 0.5
    LORA_SCALE = 16.0 / 16.0 ** 0.5
    EPS = 1e-5
    WC = w_all.shape[1]
    VCUT = 18
    COLS = [(0, E), (E, 2 * E), (2 * E, 2 * E + VCUT * D), (2 * E + VCUT * D, WC)]
    MID = (H - VCUT) * D
    MASK_ID = 163.0
    MASK_TRI = MASK / SCALE / MASK_ID
    assert NT == 2 and WC == 3 * E + ER + NE and MASK_TRI == -1632.0

    ORDER = plan(NB, NU)
    place = {step: i for i, step in enumerate(ORDER)}
    nth, seen, misc_no, banked = {}, {}, {}, 0
    for step in ORDER:
        nth[step] = seen.get(step[0], 0)
        seen[step[0]] = nth[step] + 1
        first = step[0] not in ("proj", "wo") or step[-1] == 0
        if step[0] in ("xt", "proj", "qkt", "otok", "ctxt", "gmt", "delta", "wo", "mt") and first:
            misc_no[step] = banked
            banked += 1
        elif not first:
            misc_no[step] = misc_no[step[:-1] + (0,)]

    with ExitStack() as ctx:
        def sb(name, shape, dt=F32):
            return ctx.enter_context(nc.sbuf_tensor(name, shape, dt))

        def psum(name):
            return ctx.enter_context(nc.psum_tensor(name, [P, 512], F32))

        def sem(name):
            return ctx.enter_context(nc.semaphore(name))

        xs = sb("xs", [P, NB, NT, E])
        xn = sb("xn", [P, NT, E])
        x_hi = sb("x_hi", [P, NT, KC, P], F32R)
        x_lo = sb("x_lo", [P, NT, KC, P], F32R)
        w_hi = sb("w_hi", [P, KC, WC], F32R)
        w_lo = sb("w_lo", [P, KC, WC], F32R)
        wo_hi = sb("wo_hi", [P, KC, E], F32R)
        wo_lo = sb("wo_lo", [P, KC, E], F32R)
        VC = WC - 2 * E
        bias_rows = sb("bias_rows", [98, VC], F32R)
        ones_rows = sb("ones_rows", [98, P], F32R)
        ones_b = sb("ones_b", [3, S], BF16)
        expert_hi = sb("expert_hi", [2 * ER, E], F32R)
        expert_lo = sb("expert_lo", [ER, E], F32R)
        rope_t = sb("rope_t", [P, NT, 2, D])
        cos_t, sin_t = rope_t[:, :, 0, :], rope_t[:, :, 1, :]
        qk_rot = sb("qk_rot", [P, NT, 2, E])
        rope_sin_part = sb("rope_sin_part", [P, 2, E])
        parts = sb("parts", [P, 6, 4, S], BF16)
        part_rest = sb("part_rest", [P, E])
        stack = sb("stack", [P, 2, H, S], BF16)
        v_ones = sb("v_ones", [P, 2, NT, H, D + 1])
        probs = sb("probs", [P, 6, 512])
        o_t = sb("o_t", [P, NU, S])
        ctx_n = sb("ctx_n", [P, NT, E])
        ctx_hi = sb("ctx_hi", [P, KC, P], F32R)
        ctx_lo = sb("ctx_lo", [P, KC, P], F32R)
        fin = sb("fin", [P, 2, E])
        ident = sb("ident", [P, P])
        ident_b = sb("ident_b", [P, P], BF16)
        mask_id = sb("mask_id", [P, P], BF16)
        tri_row = sb("tri_row", [P, P], BF16)
        tri_col = sb("tri_col", [P, P], BF16)
        ln_st = sb("ln_st", [P, NT, 6])
        ln_mv = sb("ln_mv", [P, NT, 2])
        ln_ve = sb("ln_ve", [P, NT, 1])
        ln_rs = sb("ln_rs", [P, NT, 1])
        neg_half = sb("neg_half", [P, NT, 1])
        mx = sb("mx", [P, 2, NT, 8])
        m_parts = sb("m_parts", [P, 2, NT, 3, 8], BF16)
        m_rest = sb("m_rest", [P, NT, 8])
        m_rows = sb("m_rows", [24, 2, S], BF16)
        NMISC = 3
        rsum = sb("rsum", [P, NMISC, 16])
        ar = sb("ar", [P, 2, NT, ER + NE])
        before = sb("before", [P, NE, NE])
        g_gt = sb("g_gt", [P, NT, NE, NE])
        g_eq = sb("g_eq", [P, NT, NE, NE])
        g_rank = sb("g_rank", [P, NT, NE])
        g_max = sb("g_max", [P, NT, 1])
        g_exp = sb("g_exp", [P, NT, NE])
        g_sum = sb("g_sum", [P, NT, 1])
        gm_raw = sb("gm_raw", [P, NT, ER])
        gm = sb("gm", [P, NT, 2, ER], F32R)
        gm_t = sb("gm_t", [2 * ER, S], F32R)

        w_raw = stack[:, :, :, :].rearrange("p a h s -> p (a h s)").bitcast(F32)
        wo_raw = probs[:, :, :].rearrange("p a n -> p (a n)")[:, 0:KC * E].rearrange("p (k n) -> p k n", k=KC)
        expert_raw = ctx_n[:, 0, :]
        BC = 4 * E // P
        bias_raw, bias_hi, bias_lo = o_t[:, 0, 0:BC], o_t[:, 0, BC:2 * BC], o_t[:, 0, 2 * BC:3 * BC]
        WP, at = [], 0
        for c0, c1 in ((0, E), (E, 2 * E), (2 * E, WC)):
            for k in range(0, KC, 2):
                raw = w_raw[:, at:at + 2 * (c1 - c0)].rearrange("p (k n) -> p k n", k=2)
                WP.append((raw, w_hi[:, k:k + 2, c0:c1], w_lo[:, k:k + 2, c0:c1], (c0, c1), k))
                at += 2 * (c1 - c0)
        for k in range(0, KC, 2):
            WP.append((wo_raw[:, k:k + 2, :], wo_hi[:, k:k + 2, :], wo_lo[:, k:k + 2, :], None, k))
        NWQ = len(WP) - 2

        row_bank = [psum("row_bank0"), psum("row_bank1")]
        t_bank = [psum("t_bank0"), psum("t_bank1")]
        o_bank = psum("o_bank")
        misc_bank = [psum(f"misc_bank{i}") for i in range(NMISC)]

        x_in = [sem(f"x_in{f}") for f in range(NT)] + [sem(f"x_in_row{b}") for b in range(1, NB)]
        w_in = [sem(f"w_in{i}") for i in range(len(WP))]
        bias_in, eb_in, rope_in = sem("bias_in"), sem("eb_in"), sem("rope_in")
        eb_hi_done, eb_lo_done = sem("eb_hi_done"), sem("eb_lo_done")
        ident_ready, masks_ready, v_ones_ready = sem("ident_ready"), sem("masks_ready"), sem("v_ones_ready")
        stack_ones, ones_b_ready = sem("stack_ones"), sem("ones_b_ready")
        w_hi_done = sem("w_hi_done")
        w_lo_done = [sem(f"w_lo_done{i}") for i in range(len(WP))]
        bias_split, bias_rows_in, zeros_ready = sem("bias_split"), sem("bias_rows_in"), sem("zeros_ready")
        dve_step = sem("dve_step")
        pool_step = sem("pool_step")
        stats_ready, rstd_ready, xn_ready = sem("stats_ready"), sem("rstd_ready"), sem("xn_ready")
        xh_ready, ar_v_ready = sem("xh_ready"), sem("ar_v_ready")
        misc_full = [sem(f"misc_full{i}") for i in range(NMISC)]
        misc_free = [sem(f"misc_free{i}") for i in range(NMISC)]
        rope_done = sem("rope_done")
        qh_ready, parts_ready = sem("qh_ready"), sem("parts_ready")
        stack_in = [sem(f"stack_in{u}") for u in range(NU)]
        row_full, row_max = sem("row_full"), sem("row_max")
        mp_ready = sem("mp_ready")
        m_in = [sem("m_in0"), sem("m_in1")]
        t_full, exp_done = sem("t_full"), sem("exp_done")
        o_full, o_copied = sem("o_full"), sem("o_copied")
        o_zeroed = sem("o_zeroed")
        ch_ready = sem("ch_ready")
        gate_dl, gate_exp, gm_ready = sem("gate_dl"), sem("gate_exp"), sem("gm_ready")
        tanh_done, out_ready = sem("tanh_done"), sem("out_ready")
        stored = [sem("stored0"), sem("stored1")]

        def misc(step):
            return misc_bank[misc_no[step] % NMISC]

        def last_proj(b, t):
            return max((("proj", b, t, c, KC - 1) for c in range(4)), key=place.get)

        def ctx_parts(step):
            _, b, t, half = step
            hi, lo = (x_hi[:, t, :, :], x_lo[:, t, :, :]) if b == NB - 1 else (ctx_hi[:, :, :], ctx_lo[:, :, :])
            return hi[:, 2 * half:2 * half + 2, :], lo[:, 2 * half:2 * half + 2, :]

        def misc_freed(step):
            return misc_free[misc_no[step] % NMISC]

        def wait_misc_full(eng, step):
            eng.wait_ge(misc_full[misc_no[step] % NMISC], misc_no[step] // NMISC + 1)

        def wait_misc_free(eng, step):
            if misc_no[step] >= NMISC:
                eng.wait_ge(misc_freed(step), misc_no[step] // NMISC)

        def wait_misc_read(eng, step):
            eng.wait_ge(misc_freed(step), misc_no[step] // NMISC + 1)

        rope_no = {step: i for i, step in enumerate(s for s in ORDER if s[0] == "proj" and s[3] < 2 and s[4] == KC - 1)}

        block = ctx.enter_context(nc.Block())

        @block.sync
        def _(sp):
            x_v = x.rearrange("b (t p) e -> b p t e", p=P)
            w_v = w_all.rearrange("(k p) n -> p k n", p=P)
            for t in range(NT):
                sp.dma_start(xs[:, 0, t, :], x_v[0, :, t, :]).then_inc(x_in[t], 16)
            for i, (raw, _, _, cols, k) in enumerate(WP):
                source = w_out.rearrange("(k p) n -> p k n", p=P) if cols is None else w_v[:, :, cols[0]:cols[1]]
                if i == NWQ:
                    sp.dma_start(xs[:, 1, :, :], x_v[1]).then_inc(x_in[NT], 16)
                sp.dma_start(raw, source[:, k:k + 2, :]).then_inc(w_in[i], 16)
                if i == 1:
                    sp.wait_ge(bias_split, 1)
                    for row, part in enumerate((bias_hi, bias_lo)):
                        sp.dma_start(bias_rows[row:row + 97:32, 0:E].rearrange("c (p j) -> c p j", j=BC).bitcast(F32),
                                     part).then_inc(bias_rows_in, 16)
                    sp.dma_start(rope_t[:, :, :, :], rope.rearrange("(t p) a d -> p t a d", p=P)).then_inc(rope_in, 16)
            for part in range(2):
                sp.dma_start(expert_raw[part * ER:(part + 1) * ER, :], experts_b).then_inc(eb_in, 16)
            for b in range(2, NB):
                sp.dma_start(xs[:, b, :, :], x_v[b]).then_inc(x_in[NT + b - 1], 16)
            for i in range(NWQ):
                sp.wait_ge(w_lo_done[i], 1)
            sp.wait_ge(ones_b_ready, 1)
            sp.dma_start(stack[96:99, 1, :, :],
                         ones_b[:, :].unsqueeze(1).broadcast_to([3, H, S])).then_inc(stack_ones, 16)

            for step in ORDER:
                kind = step[0]
                if kind == "stack":
                    _, b, u = step
                    sp.wait_ge(parts_ready, 4 * (b + 1))
                    if b:
                        sp.wait_ge(t_full, 3 * (NU * (b - 1) + u + 1))
                    for slot, (qp, kp) in enumerate(((0, 0), (0, 1), (0, 2), (1, 0), (1, 1), (2, 0))):
                        sp.dma_start(stack[D * slot:D * (slot + 1), :, 4 * u:4 * u + 4, :],
                                     parts[D * u:D * (u + 1), qp:4 + kp:3 + kp - qp, :, :]).then_inc(stack_in[u], 16)
                if kind == "wo" and step[3] == KC - 1:
                    _, b, t, k = step
                    f = NT * b + t
                    sp.wait_ge(out_ready, f + 1)
                    sp.dma_start(out[b, t * P:(t + 1) * P, :], fin[:, f % 2, :]).then_inc(stored[f % 2], 16)
            for q in stored:
                sp.wait_ge(q, 16 * (NB * NT // 2))

        @block.gpsimd
        def _(pool):
            n = [0]

            def link(ins):
                n[0] += 1
                ins.then_inc(pool_step, 1)
                pool.wait_ge(pool_step, n[0])

            def masked(tile, value, op, step, mult):
                link(pool.memset(tile[:, :], value))
                return pool.affine_select(out=tile[:, :], in_=tile[:, :], compare_op=op, fill=0.0, base=0,
                                          pattern=[[step, tile.shape[1]]], channel_multiplier=mult)

            link(pool.memset(neg_half[:, :, :], -0.5))
            masked(ident, 1.0, ALU.is_equal, -1, 1).then_inc(ident_ready, 1)
            pool.memset(ones_rows[:, :].bitcast(F32), 1.0).then_inc(zeros_ready, 1)
            masked(ident_b, 1.0, ALU.is_equal, -1, 1).then_inc(masks_ready, 1)
            masked(mask_id, MASK_ID, ALU.is_equal, -1, 1).then_inc(masks_ready, 1)
            masked(tri_row, MASK_TRI, ALU.is_gt, -1, 1).then_inc(masks_ready, 1)
            masked(tri_col, MASK_TRI, ALU.is_gt, 1, -1).then_inc(masks_ready, 1)
            pool.memset(ones_b[:, :], 1.0).then_inc(ones_b_ready, 1)
            pool.memset(v_ones[:, :, :, :, D:D + 1].rearrange("p a t h d -> p (a t h) d"),
                        1.0).then_inc(v_ones_ready, 1)

            for step in ORDER:
                kind = step[0]
                if kind == "ln_stats":
                    _, b, t = step
                    pool.wait_ge(stats_ready, nth[step] + 1)
                    link(pool.tensor_scalar(ln_ve[:, t, :], ln_mv[:, t, 1:2], EPS, None, ALU.add))
                    pool.tensor_tensor(ln_rs[:, t, :], ln_ve[:, t, :], neg_half[:, t, :],
                                       ALU.pow).then_inc(rstd_ready, 1)
                if kind == "weights" and step[2] >= 4:
                    i = step[2]
                    raw, hi, lo, _, _ = WP[i]
                    pool.wait_ge(w_hi_done, i + 1)
                    pool.tensor_tensor(lo, raw, hi.bitcast(F32), ALU.subtract).then_inc(w_lo_done[i], 1)
                if kind == "proj" and step[3] < 2 and step[4] == KC - 1:
                    _, b, t, w, k = step
                    r = rope_no[step]
                    wait_misc_read(pool, step)
                    pool.tensor_tensor(qk_rot[:, t, w, :], qk_rot[:, t, w, :], rope_sin_part[:, r % 2, :],
                                       ALU.add).then_inc(rope_done, 1)
                if kind == "wo" and step[3] == KC - 1:
                    _, b, t, k = step
                    f = NT * b + t
                    wait_misc_read(pool, step)
                    pool.tensor_tensor(fin[:, f % 2, :], fin[:, f % 2, :], xs[:, b, t, :],
                                       ALU.add).then_inc(out_ready, 1)

        @block.scalar
        def _(act):
            act.dma_start(bias_raw, bias.rearrange("o (p j) -> (o p) j", p=P)).then_inc(bias_in, 16)
            for step in ORDER:
                kind = step[0]
                if kind == "experts":
                    act.wait_ge(eb_in, 32)
                    nc.scalar.activation(expert_hi[:, :], expert_raw, ACT.Copy).then_inc(eb_hi_done, 1)
                if kind == "weights":
                    raw, hi, lo, _, _ = WP[step[2]]
                    act.wait_ge(w_in[step[2]], 16)
                    nc.scalar.activation(hi, raw, ACT.Copy).then_inc(w_hi_done, 1)
                if kind == "xt":
                    _, b, t = step
                    wait_misc_full(act, step)
                    if b:
                        wait_misc_full(act, last_proj(b - 1, t))
                    nc.scalar.activation(x_hi[:, t, :, :], misc(step)[:, :].rearrange("p (k n) -> p k n", k=KC),
                                         ACT.Copy).then_inc(xh_ready, 1)
                if kind == "qkt":
                    _, b, t, w = step
                    wait_misc_full(act, step)
                    if b and nth[step] % 4 == 0:
                        for u in range(NU):
                            act.wait_ge(stack_in[u], 96 * b)
                    nc.scalar.activation(parts[:, 3 * w, :, t * P:(t + 1) * P],
                                         misc(step)[:, :].rearrange("p (g n) -> p g n", g=4),
                                         ACT.Copy).then_inc(qh_ready, 1)
                if kind == "proj" and step[3] >= 2 and step[4] == KC - 1:
                    _, b, t, c, k = step
                    wait_misc_full(act, step)
                    if b >= 2:
                        act.wait_ge(o_full, NU * (b - 1))
                    elif b == 0:
                        act.wait_ge(v_ones_ready, 1)
                    h0, h1 = (0, VCUT) if c == 2 else (VCUT, H)
                    cols = (h1 - h0) * D
                    if c == 3:
                        nc.scalar.activation(ar[:, b % 2, t, :], misc(step)[:, cols:cols + ER + NE],
                                             ACT.Copy).then_inc(ar_v_ready, 1)
                    nc.scalar.activation(v_ones[:, b % 2, t, h0:h1, 0:D],
                                         misc(step)[:, 0:cols].rearrange("p (h d) -> p h d", d=D),
                                         ACT.Copy).then_inc(misc_freed(step), 1)
                if kind == "mt":
                    s = step[1]
                    b, g = s // NG, s % NG
                    wait_misc_full(act, step)
                    if s >= 2:
                        act.wait_ge(m_in[s % 2], 16 * (s // 2))
                    nc.scalar.activation(m_rows[:, s % 2, :], misc(step)[0:24, 0:P].bitcast(BF16),
                                         ACT.Copy).then_inc(misc_freed(step), 1)
                    wait_misc_read(act, step)
                    if b:
                        act.wait_ge(t_full, 3 * (NU * (b - 1) + 2 * g + 2))
                    act.dma_start(stack[96:99, 0, 8 * g:8 * g + 8, :], m_rows[:, s % 2, :]).then_inc(m_in[s % 2], 16)
                if kind == "tt":
                    n = step[1]
                    U = n // 3
                    act.wait_ge(t_full, n + 1)
                    if U >= 2 and n % 3 == 0:
                        act.wait_ge(o_full, U - 1)
                    if n == 0:
                        for i in range(NWQ, len(WP)):
                            act.wait_ge(w_lo_done[i], 1)
                    nc.scalar.activation(probs[:, n % 6, :], t_bank[n % 2][:, :], ACT.Exp,
                                         scale=SCALE).then_inc(exp_done, 1)
                if kind == "ov":
                    U = step[1]
                    b, u = U // NU, U % NU
                    act.wait_ge(o_full, U + 1)
                    if b:
                        wait_misc_full(act, ("otok", b - 1, u // 4, 1))
                    elif u == 0:
                        act.wait_ge(bias_rows_in, 32)
                    nc.scalar.activation(o_t[:, u, :], o_bank[:, 0:S], ACT.Copy).then_inc(o_copied, 1)
                if kind == "ctxt":
                    _, b, t, half = step
                    wait_misc_full(act, step)
                    f = NT * b + t
                    if b == NB - 1:
                        wait_misc_full(act, last_proj(b, t))
                    elif f:
                        wait_misc_full(act, ("wo", (f - 1) // NT, (f - 1) % NT, 0))
                    nc.scalar.activation(ctx_parts(step)[0], misc(step)[:, 0:256].rearrange("p (k n) -> p k n", k=2),
                                         ACT.Copy).then_inc(ch_ready, 1)
                if kind == "gate_a":
                    b = step[1]
                    act.wait_ge(gate_dl, b + 1)
                    nc.scalar.activation(g_exp[:, :, :], g_exp[:, :, :], ACT.Exp).then_inc(gate_exp, 1)
                if kind == "delta":
                    _, b, t = step
                    f = NT * b + t
                    wait_misc_full(act, step)
                    if f >= 2:
                        act.wait_ge(stored[f % 2], 16 * (f // 2))
                    nc.scalar.activation(fin[:, f % 2, :], misc(step)[:, :], ACT.Tanh,
                                         scale=0.5).then_inc(tanh_done, 1)

        @block.vector
        def _(dve):
            n = [0]

            def link(ins):
                n[0] += 1
                ins.then_inc(dve_step, 1)
                dve.wait_ge(dve_step, n[0])

            link(dve.memset(before[:, :, :], 0.0))
            for e in range(1, NE):
                last = dve.memset(before[:, e, 0:e], 1.0)
            link(last)
            dve.memset(bias_rows[64:66, E:VC].bitcast(F32), 0.0).then_inc(zeros_ready, 1)
            dve.memset(o_bank[:, 0:S], 0.0).then_inc(o_zeroed, 1)

            for step in ORDER:
                kind = step[0]
                if kind == "bias":
                    dve.wait_ge(bias_in, 16)
                    link(dve.tensor_copy(bias_hi.bitcast(F32R), bias_raw))
                    dve.tensor_tensor(bias_lo.bitcast(F32R), bias_raw, bias_hi, ALU.subtract).then_inc(bias_split, 1)
                if kind == "experts":
                    dve.wait_ge(eb_hi_done, 1)
                    dve.tensor_tensor(expert_lo[:, :], expert_raw[0:ER, :], expert_hi[0:ER, :].bitcast(F32),
                                      ALU.subtract).then_inc(eb_lo_done, 1)
                if kind == "weights" and step[2] < 4:
                    i = step[2]
                    raw, hi, lo, _, _ = WP[i]
                    dve.wait_ge(w_hi_done, i + 1)
                    dve.tensor_tensor(lo, raw, hi.bitcast(F32), ALU.subtract).then_inc(w_lo_done[i], 1)
                if kind == "ln_stats":
                    _, b, t = step
                    dve.wait_ge(x_in[b + NT - 1] if b else x_in[t], 16)
                    link(dve.bn_stats(ln_st[:, t, :], xs[:, b, t, :]))
                    dve.bn_aggr(ln_mv[:, t, :], ln_st[:, t, :]).then_inc(stats_ready, 1)
                if kind == "ln_apply":
                    _, b, t = step
                    dve.wait_ge(rstd_ready, nth[step] + 1)
                    dve.tensor_scalar(xn[:, t, :], xs[:, b, t, :], ln_mv[:, t, 0:1], ln_rs[:, t, 0:1],
                                      ALU.subtract, ALU.mult).then_inc(xn_ready, 1)
                if kind == "xt":
                    _, b, t = step
                    dve.wait_ge(xh_ready, nth[step] + 1)
                    dve.tensor_tensor(x_lo[:, t, :, :], misc(step)[:, :].rearrange("p (k n) -> p k n", k=KC),
                                      x_hi[:, t, :, :].bitcast(F32), ALU.subtract).then_inc(misc_freed(step), 1)
                if kind == "proj" and step[3] < 2 and step[4] == KC - 1:
                    _, b, t, w, k = step
                    r = rope_no[step]
                    wait_misc_full(dve, step)
                    if r == 0:
                        dve.wait_ge(rope_in, 16)
                    if r >= 2:
                        dve.wait_ge(rope_done, r - 1)
                    q = misc(step)[:, :].rearrange("p (h d) -> p h d", d=D)
                    dve.tensor_tensor(qk_rot[:, t, w, :].rearrange("p (h d) -> p h d", d=D), q,
                                      cos_t[:, t:t + 1, :].broadcast_to([P, H, D]), ALU.mult)
                    dve.tensor_tensor(
                        rope_sin_part[:, r % 2, :].rearrange("p (h a d) -> p h a d", a=2, d=HALF),
                        misc(step)[:, :].rearrange("p (h a d) -> p h a d", a=2, d=HALF)[:, :, ::-1, :],
                        sin_t[:, t, :].rearrange("p (a d) -> p a d", a=2).unsqueeze(1).broadcast_to([P, H, 2, HALF]),
                        ALU.mult).then_inc(misc_freed(step), 1)
                if kind == "qkt":
                    _, b, t, w = step
                    r = nth[step]
                    dve.wait_ge(qh_ready, r + 1)
                    if r:
                        dve.wait_ge(parts_ready, r)
                    rest = part_rest[:, :].rearrange("p (g n) -> p g n", g=4)
                    pw = parts[:, 3 * w:3 * w + 3, :, t * P:(t + 1) * P]
                    dve.tensor_tensor(rest, misc(step)[:, :].rearrange("p (g n) -> p g n", g=4), pw[:, 0, :, :],
                                      ALU.subtract).then_inc(misc_freed(step), 1)
                    wait_misc_read(dve, step)
                    link(dve.tensor_copy(pw[:, 1, :, :], rest))
                    dve.tensor_tensor(pw[:, 2, :, :], rest, pw[:, 1, :, :], ALU.subtract).then_inc(parts_ready, 1)
                if kind == "row":
                    n_ = step[1]
                    U, i = n_ // 3, n_ % 3
                    m, o = mx[:, U // 2 % 2, :, :], 4 * (U % 2)
                    t, h0, h1 = (0, o, o + 4) if i == 0 else (1, o + 2 * i - 2, o + 2 * i)
                    dve.wait_ge(row_full, n_ + 1)
                    dve.tensor_reduce(m[:, t, h0:h1], row_bank[n_ % 2][:, :].rearrange("p (h n) -> p h n", h=h1 - h0),
                                      AX.X, ALU.max).then_inc(row_max, 1)
                if kind == "msplit":
                    s = step[1]
                    dve.wait_ge(row_max, 6 * (s + 1))
                    if s >= 2:
                        wait_misc_full(dve, ("mt", s - 2))
                    m, mp = mx[:, s % 2, :, :], m_parts[:, s % 2, :, :, :]
                    link(dve.tensor_scalar(mp[:, :, 0, :], m, -1.0, None, ALU.mult))
                    link(dve.scalar_tensor_tensor(m_rest[:, :, :], m, -1.0, mp[:, :, 0, :], ALU.mult, ALU.subtract))
                    link(dve.tensor_copy(mp[:, :, 1, :], m_rest[:, :, :]))
                    dve.tensor_tensor(mp[:, :, 2, :], m_rest[:, :, :], mp[:, :, 1, :],
                                      ALU.subtract).then_inc(mp_ready, 1)
                if kind == "otok":
                    _, b, half, t = step
                    wait_misc_full(dve, step)
                    o = misc(step)[:, :].rearrange("p (h d) -> p h d", d=2 * D)
                    per_head = rsum[:, misc_no[step] % NMISC, :].rearrange("p (h d) -> p h d", d=1)
                    link(dve.reciprocal(per_head, o[:, :, D:D + 1]))
                    dve.tensor_tensor(
                        ctx_n[:, t, half * 256:(half + 1) * 256].rearrange("p (h d) -> p h d", d=D), o[:, :, 0:D],
                        per_head.broadcast_to([P, 16, D]), ALU.mult).then_inc(misc_freed(step), 1)
                if kind == "ctxt":
                    hi, lo = ctx_parts(step)
                    dve.wait_ge(ch_ready, nth[step] + 1)
                    dve.tensor_tensor(lo, misc(step)[:, 0:256].rearrange("p (k n) -> p k n", k=2), hi.bitcast(F32),
                                      ALU.subtract).then_inc(misc_freed(step), 1)
                if kind == "gate_a":
                    b = step[1]
                    dve.wait_ge(ar_v_ready, NT * (b + 1))
                    lg = ar[:, b % 2, :, ER:ER + NE]
                    for t in range(NT):
                        of_j = lg[:, t:t + 1, :].broadcast_to([P, NE, NE])
                        of_e = lg[:, t, :].unsqueeze(2).broadcast_to([P, NE, NE])
                        dve.tensor_tensor(g_gt[:, t, :, :], of_j, of_e, ALU.is_gt)
                        last = dve.tensor_tensor(g_eq[:, t, :, :], of_j, of_e, ALU.is_equal)
                    link(last)
                    for t in range(NT):
                        last = dve.tensor_tensor(g_eq[:, t, :, :], g_eq[:, t, :, :], before[:, :, :], ALU.mult)
                    link(last)
                    link(dve.tensor_tensor(g_gt[:, :, :, :], g_gt[:, :, :, :], g_eq[:, :, :, :], ALU.add))
                    dve.tensor_reduce(g_rank[:, :, :], g_gt[:, :, :, :], AX.X, ALU.add)
                    link(dve.tensor_reduce(g_max[:, :, :], lg, AX.X, ALU.max))
                    dve.tensor_tensor(g_exp[:, :, :], lg, g_max[:, :, :].broadcast_to([P, NT, NE]),
                                      ALU.subtract).then_inc(gate_dl, 1)
                if kind == "gate_b":
                    b = step[1]
                    dve.wait_ge(gate_exp, b + 1)
                    link(dve.scalar_tensor_tensor(g_exp[:, :, :], g_rank[:, :, :], 2.0, g_exp[:, :, :], ALU.is_lt,
                                                  ALU.mult))
                    link(dve.tensor_reduce(g_sum[:, :, :], g_exp[:, :, :], AX.X, ALU.add))
                    link(dve.reciprocal(g_sum[:, :, :], g_sum[:, :, :]))
                    link(dve.scalar_tensor_tensor(g_exp[:, :, :], g_exp[:, :, :], LORA_SCALE,
                                                  g_sum[:, :, :].broadcast_to([P, NT, NE]), ALU.mult, ALU.mult))
                    for t in range(NT):
                        last = dve.tensor_tensor(gm_raw[:, t, :].rearrange("p (e r) -> p e r", r=R),
                                                 ar[:, b % 2, t, 0:ER].rearrange("p (e r) -> p e r", r=R),
                                                 g_exp[:, t, :].unsqueeze(2).broadcast_to([P, NE, R]), ALU.mult)
                    link(last)
                    link(dve.tensor_copy(gm[:, :, 0, :], gm_raw[:, :, :]))
                    dve.tensor_tensor(gm[:, :, 1, :], gm_raw[:, :, :], gm[:, :, 0, :].bitcast(F32),
                                      ALU.subtract).then_inc(gm_ready, 1)
                if kind == "gmt":
                    wait_misc_full(dve, step)
                    dve.tensor_copy(gm_t[:, :], misc(step)[:, 0:S]).then_inc(misc_freed(step), 1)
                if kind == "delta":
                    _, b, t = step
                    f = NT * b + t
                    dve.wait_ge(tanh_done, f + 1)
                    dve.scalar_tensor_tensor(fin[:, f % 2, :], fin[:, f % 2, :], 1.0, misc(step)[:, :], ALU.add,
                                             ALU.mult).then_inc(misc_freed(step), 1)
                if kind == "wo" and step[3] == KC - 1:
                    _, b, t, k = step
                    f = NT * b + t
                    wait_misc_full(dve, step)
                    wait_misc_read(dve, ("delta", b, t))
                    dve.scalar_tensor_tensor(fin[:, f % 2, :], fin[:, f % 2, :], 0.5, misc(step)[:, :], ALU.mult,
                                             ALU.mult).then_inc(misc_freed(step), 1)

        @block.tensor
        def _(pe):
            def three_passes(step, k, cols, hi, lo, rhs_hi, rhs_lo, bias_row, bias_at):
                bank = misc(step)[:, 0:cols]
                pe.matmul(bank, hi, rhs_hi, start=(k == 0), stop=False)
                pe.matmul(bank, hi, rhs_lo, start=False, stop=False)
                last = pe.matmul(bank, lo, rhs_hi, start=False, stop=False)
                if k == KC - 1:
                    if nth[step] == KC - 1 and step[0] == "proj":
                        pe.wait_ge(zeros_ready, 2)
                        pe.wait_ge(bias_rows_in, 32)
                    last = pe.matmul(bank, ones_rows[bias_row:bias_row + 2, :],
                                     bias_rows[bias_row:bias_row + 2, bias_at:bias_at + cols], start=False, stop=True)
                    last.then_inc(misc_full[misc_no[step] % NMISC], 1)

            for step in ORDER:
                kind = step[0]
                if step in misc_no and (kind not in ("proj", "wo") or step[-1] == 0):
                    wait_misc_free(pe, step)
                if kind == "xt":
                    _, b, t = step
                    if b == 0 and t == 0:
                        pe.wait_ge(ident_ready, 1)
                    pe.wait_ge(xn_ready, nth[step] + 1)
                    for k in range(KC):
                        last = pe.transpose(misc(step)[:, k * P:(k + 1) * P], xn[:, t, k * P:(k + 1) * P], ident[:, :])
                    last.then_inc(misc_full[misc_no[step] % NMISC], 1)
                if kind == "proj":
                    _, b, t, c, k = step
                    if k == 0:
                        wait_misc_read(pe, ("xt", b, t))
                    if b == 0 and k % 2 == 0:
                        pe.wait_ge(w_lo_done[2 * min(c, 2) + k // 2], 1)
                    c0, c1 = COLS[c]
                    three_passes(step, k, c1 - c0, x_hi[:, t, k, :], x_lo[:, t, k, :], w_hi[:, k, c0:c1],
                                 w_lo[:, k, c0:c1], 32 * min(c, 2), c0 - E * min(c, 2))
                if kind == "qkt":
                    _, b, t, w = step
                    pe.wait_ge(rope_done, rope_no[("proj", b, t, w, KC - 1)] + 1)
                    for g in range(4):
                        last = pe.transpose(misc(step)[:, g * P:(g + 1) * P], qk_rot[:, t, w, g * P:(g + 1) * P],
                                            ident[:, :])
                    last.then_inc(misc_full[misc_no[step] % NMISC], 1)
                if kind == "row":
                    n = step[1]
                    U, i = n // 3, n % 3
                    b, u = U // NU, U % NU
                    pe.wait_ge(stack_in[u], 96 * (b + 1))
                    if n == 0:
                        pe.wait_ge(masks_ready, 4)
                    if n >= 2:
                        pe.wait_ge(row_max, n - 1)
                    heads = range(4) if i == 0 else range(2 * i - 2, 2 * i)
                    t = 0 if i == 0 else 1
                    bank = row_bank[n % 2][:, :].rearrange("p (h n) -> p h n", h=len(heads))
                    width = 512 // len(heads)
                    pe.matmul(bank[:, :, t * P:(t + 1) * P], tri_row[:, :],
                              mask_id[:, :].unsqueeze(1).broadcast_to([P, len(heads), P]), start=True, stop=False,
                              skip_group_check=True)
                    for j, h in enumerate(heads):
                        last = pe.matmul(bank[:, j, :], stack[0:96, 0, 4 * u + h, t * P:(t + 1) * P],
                                         stack[0:96, 1, 4 * u + h, 0:width], start=False, stop=True,
                                         skip_group_check=True)
                    last.then_inc(row_full, 1)
                if kind == "mt":
                    s = step[1]
                    pe.wait_ge(mp_ready, s + 1)
                    for t in range(NT):
                        last = pe.transpose(misc(step)[0:24, t * 64:(t + 1) * 64].bitcast(BF16),
                                            m_parts[:, s % 2, t, :, :].rearrange("p a h -> p (a h)"), ident_b[:, :])
                    last.then_inc(misc_full[misc_no[step] % NMISC], 1)
                if kind == "tt":
                    n = step[1]
                    U, i = n // 3, n % 3
                    b, u, s = U // NU, U % NU, U // 2
                    pe.wait_ge(m_in[s % 2], 16 * (s // 2 + 1))
                    if n == 0:
                        pe.wait_ge(stack_ones, 16)
                    if n >= 2:
                        pe.wait_ge(exp_done, n - 1)
                    heads = range(4) if i == 2 else range(2 * i, 2 * i + 2)
                    kb, q0 = (1, P) if i == 2 else (0, 0)
                    bank = t_bank[n % 2][:, :].rearrange("p (h n) -> p h n", h=len(heads))
                    pe.matmul(bank[:, :, 0:P], tri_col[:, :],
                              mask_id[:, :].unsqueeze(1).broadcast_to([P, len(heads), P]), start=True, stop=False,
                              skip_group_check=True)
                    for j, h in enumerate(heads):
                        last = pe.matmul(bank[:, j, :], stack[0:99, 1, 4 * u + h, kb * P:(kb + 1) * P],
                                         stack[0:99, 0, 4 * u + h, q0:S], start=False, stop=True,
                                         skip_group_check=True)
                    last.then_inc(t_full, 1)
                if kind == "pv":
                    U = step[1]
                    b, u = U // NU, U % NU
                    pe.wait_ge(exp_done, 3 * U + 3)
                    if u == 0:
                        for t in range(NT):
                            for c in (2, 3):
                                wait_misc_read(pe, ("proj", b, t, c, KC - 1))
                    if U == 0:
                        pe.wait_ge(o_zeroed, 1)
                    else:
                        pe.wait_ge(o_copied, U)
                    for kb in range(2):
                        for h in range(4):
                            n = 3 * U + (2 if kb else h // 2)
                            width = S - kb * P
                            at = h * width if kb else (h % 2) * width
                            last = pe.matmul(o_bank[32 * h:32 * h + D + 1, kb * P:S],
                                             v_ones[:, b % 2, kb, 8 * h + u, :],
                                             probs[:, n % 6, at:at + width], start=(kb == 0), stop=(kb == 1),
                                             skip_group_check=True)
                    last.then_inc(o_full, 1)
                if kind == "otok":
                    _, b, half, t = step
                    pe.wait_ge(o_copied, NU * b + 4 * half + 4)
                    for j in range(4):
                        last = pe.transpose(misc(step)[:, j * P:(j + 1) * P],
                                            o_t[:, 4 * half + j, t * P:(t + 1) * P], ident[:, :])
                    last.then_inc(misc_full[misc_no[step] % NMISC], 1)
                if kind == "ctxt":
                    _, b, t, half = step
                    wait_misc_read(pe, ("otok", b, half, t))
                    for k in range(2):
                        last = pe.transpose(misc(step)[:, k * P:(k + 1) * P],
                                            ctx_n[:, t, (2 * half + k) * P:(2 * half + k + 1) * P], ident[:, :])
                    last.then_inc(misc_full[misc_no[step] % NMISC], 1)
                if kind == "gmt":
                    b = step[1]
                    pe.wait_ge(gm_ready, b + 1)
                    for t in range(NT):
                        last = pe.transpose(misc(step)[:, t * P:(t + 1) * P],
                                            gm[:, t, :, :].rearrange("p a r -> p (a r)").bitcast(F32), ident[:, :])
                    last.then_inc(misc_full[misc_no[step] % NMISC], 1)
                if kind == "delta":
                    _, b, t = step
                    wait_misc_read(pe, ("gmt", b))
                    if b == 0:
                        pe.wait_ge(eb_lo_done, 1)
                    tokens = slice(t * P, (t + 1) * P)
                    pe.matmul(misc(step)[:, :], gm_t[:, tokens], expert_hi[:, :], start=True, stop=False)
                    pe.matmul(misc(step)[:, :], gm_t[0:ER, tokens], expert_lo[:, :], start=False,
                              stop=True).then_inc(misc_full[misc_no[step] % NMISC], 1)
                if kind == "wo":
                    _, b, t, k = step
                    if k % 2 == 0:
                        wait_misc_read(pe, ("ctxt", b, t, k // 2))
                    if b == 0 and k % 2 == 0:
                        pe.wait_ge(w_lo_done[NWQ + k // 2], 1)
                    hi, lo = ctx_parts(("ctxt", b, t, k // 2))
                    three_passes(step, k, E, hi[:, k % 2, :], lo[:, k % 2, :], wo_hi[:, k, :], wo_lo[:, k, :], 96, 0)


def kernel(L0_attn_hidden_states, L0_attn_qkv_w, L0_attn_qkv_b, L0_attn_out_w, L0_attn_out_b, L0_ffn_router_w,
           L0_ffn_A, L0_ffn_B):
    import numpy as np
    import concourse.bacc as bacc
    from concourse.bass_utils import run_bass_kernel_spmd

    x = np.ascontiguousarray(L0_attn_hidden_states)
    NB, S, E = x.shape
    H, D = 32, 16
    w_all = np.concatenate([L0_attn_qkv_w, np.transpose(L0_ffn_A.reshape(-1, E)), np.transpose(L0_ffn_router_w)],
                           axis=1)
    bias = np.concatenate([L0_attn_qkv_b, L0_attn_out_b])[None, :]
    w_out = L0_attn_out_w.reshape(4, 8, D, E).transpose(1, 0, 2, 3).reshape(E, E)
    experts_b = np.transpose(L0_ffn_B, (0, 2, 1)).reshape(-1, E)
    half = D // 2
    inv_freq = (1.0 / np.float32(10000.0) ** (np.arange(half, dtype=np.float32) / np.float32(half))).astype(np.float32)
    ang = np.arange(S, dtype=np.float32)[:, None] * inv_freq[None, :]
    cos, sin = np.cos(ang).astype(np.float32), np.sin(ang).astype(np.float32)
    arrays = {
        "in_x": x, "in_w_all": w_all, "in_bias": bias, "in_w_out": w_out, "in_experts_b": experts_b,
        "in_rope": np.stack([np.concatenate([cos, cos], axis=1), np.concatenate([-sin, sin], axis=1)], axis=1),
    }
    arrays = {k: np.ascontiguousarray(v) for k, v in arrays.items()}
    nc = bacc.Bacc("TRN2", target_bir_lowering=False, num_devices=1)
    args = [nc.dram_tensor(k, v.shape, mybir.dt.from_np(v.dtype), kind="ExternalInput").ap() for k, v in arrays.items()]
    out = nc.dram_tensor("out_0", x.shape, F32, kind="ExternalOutput").ap()
    bass_attention_times_silu_lora(nc, *args, out)
    r = run_bass_kernel_spmd(nc, [arrays], core_ids=[0])
    return r.results[0]["out_0"]
```
